# Optimizing a Trainium2 kernel written in Bass

```python
import numpy as np
import jax
import jax.numpy as jnp

def _softmax(x, axis=-1):
    return jax.nn.softmax(x, axis=axis)

def _gelu(x):
    return jax.nn.gelu(x, approximate=True)

def _silu(x):
    return jax.nn.silu(x)

def _sigmoid(x):
    return jax.nn.sigmoid(x)

def _layernorm(x, axis=-1, eps=1e-05):
    m = jnp.mean(x, axis=axis, keepdims=True)
    v = jnp.var(x, axis=axis, keepdims=True)
    return (x - m) / jnp.sqrt(v + eps)

def _scatter_add(tgt, idx, src, axis=0):
    return tgt.at[idx].add(src)

def _segment_sum(src, seg, n):
    return jax.ops.segment_sum(src, seg, n)
kernel_name = 'mk_audio_tower_d1_tok_audfeat2048_r4_e97e9c'

def setup_inputs(seed: int=0):
    np.random.seed(seed)
    _w = jnp.asarray

    def _rec_inputs():
        import jax
        import jax.numpy as jnp
        _rk = jax.random.key(seed)
        x = 0.000343403 + 1.00016 * jax.random.normal(jax.random.fold_in(_rk, 1), (128, 375, 512), jnp.float32)
        return x
    x = _rec_inputs()

    def _L0_tok_setup():
        import jax, jax.numpy as jnp
        import numpy as np
        N, C3, T = (64, 192, 512)
        key = jax.random.key(seed)
        qkv = jax.random.normal(key, (N, C3, T), dtype=jnp.float32)
        return {'qkv': qkv}
    _L0_tok_all = _L0_tok_setup()
    _L0_tok_in = {k: v for k, v in _L0_tok_all.items() if k in ()}
    del _L0_tok_all

    def _L0_attn_setup():
        import jax, jax.numpy as jnp
        import numpy as np
        NUM_HEADS = 8
        NUM_KV_HEADS = 2
        HEAD_DIM = 64
        HIDDEN = 512
        ROPE_THETA = 10000.0
        QUERY_PRE_ATTN_SCALAR = 256.0
        SOFTCAP = 50.0

        def _rope_cos_sin(S, dtype):
            inv_freq = 1.0 / ROPE_THETA ** (jnp.arange(0, HEAD_DIM, 2, dtype=jnp.float32) / HEAD_DIM)
            pos = jnp.arange(S, dtype=jnp.float32)
            freqs = pos[:, None] * inv_freq[None, :]
            emb = jnp.concatenate([freqs, freqs], axis=-1)
            return (jnp.cos(emb).astype(dtype), jnp.sin(emb).astype(dtype))

        def _rotate_half(x):
            x1, x2 = (x[..., :HEAD_DIM // 2], x[..., HEAD_DIM // 2:])
            return jnp.concatenate([-x2, x1], axis=-1)
        key = jax.random.key(seed)
        k1, k2, k3, k4, k5 = jax.random.split(key, 5)
        B, S = (2, 512)
        s = 0.02
        return {'hidden_states': jax.random.normal(k1, (B, S, HIDDEN), dtype=jnp.float32), 'Wq': jax.random.normal(k2, (NUM_HEADS * HEAD_DIM, HIDDEN), dtype=jnp.float32) * s, 'Wk': jax.random.normal(k3, (NUM_KV_HEADS * HEAD_DIM, HIDDEN), dtype=jnp.float32) * s, 'Wv': jax.random.normal(k4, (NUM_KV_HEADS * HEAD_DIM, HIDDEN), dtype=jnp.float32) * s, 'Wo': jax.random.normal(k5, (HIDDEN, NUM_HEADS * HEAD_DIM), dtype=jnp.float32) * s}
    _L0_attn_all = _L0_attn_setup()
    _L0_attn_in = {k: v for k, v in _L0_attn_all.items() if k in ('Wq', 'Wk', 'Wv', 'Wo')}
    del _L0_attn_all

    def _L0_ffn_setup():
        import jax, jax.numpy as jnp
        import numpy as np
        BS, SLEN, DIM, HID, E, TOPK = (4, 512, 512, 448, 8, 2)
        key = jax.random.key(seed)
        ks = jax.random.split(key, 9)
        s = 0.02
        return {'x': jax.random.normal(ks[0], (BS, SLEN, DIM), jnp.float32), 'gate_w': jax.random.normal(ks[1], (DIM, E), jnp.float32) * s, 'w1': jax.random.normal(ks[2], (E, DIM, HID), jnp.float32) * s, 'w2': jax.random.normal(ks[3], (E, HID, DIM), jnp.float32) * s, 'w3': jax.random.normal(ks[4], (E, DIM, HID), jnp.float32) * s, 'sw1': jax.random.normal(ks[5], (DIM, HID), jnp.float32) * s, 'sw2': jax.random.normal(ks[6], (HID, DIM), jnp.float32) * s, 'sw3': jax.random.normal(ks[7], (DIM, HID), jnp.float32) * s, 'expert_bias': jnp.zeros((E,), jnp.float32)}
    _L0_ffn_all = _L0_ffn_setup()
    _L0_ffn_in = {k: v for k, v in _L0_ffn_all.items() if k in ('gate_w', 'w1', 'w2', 'w3', 'sw1', 'sw2', 'sw3', 'expert_bias')}
    del _L0_ffn_all
    return {'x': x, 'L0_attn_Wq': _L0_attn_in['Wq'], 'L0_attn_Wk': _L0_attn_in['Wk'], 'L0_attn_Wv': _L0_attn_in['Wv'], 'L0_attn_Wo': _L0_attn_in['Wo'], 'L0_ffn_gate_w': _L0_ffn_in['gate_w'], 'L0_ffn_w1': _L0_ffn_in['w1'], 'L0_ffn_w2': _L0_ffn_in['w2'], 'L0_ffn_w3': _L0_ffn_in['w3'], 'L0_ffn_sw1': _L0_ffn_in['sw1'], 'L0_ffn_sw2': _L0_ffn_in['sw2'], 'L0_ffn_sw3': _L0_ffn_in['sw3'], 'L0_ffn_expert_bias': _L0_ffn_in['expert_bias']}

def reference(x, L0_attn_Wq, L0_attn_Wk, L0_attn_Wv, L0_attn_Wo, L0_ffn_gate_w, L0_ffn_w1, L0_ffn_w2, L0_ffn_w3, L0_ffn_sw1, L0_ffn_sw2, L0_ffn_sw3, L0_ffn_expert_bias):
    import jax
    import jax.numpy as jnp

    def _L0_tok_ref(qkv):
        import jax, jax.numpy as jnp
        import numpy as np
        N, C3, T = (64, 192, 512)
        ch = qkv.shape[1] // 3
        q, k, v = jnp.split(qkv, 3, axis=1)
        scale = 1.0 / np.sqrt(np.sqrt(ch))
        weight = jnp.einsum('bct,bcs->bts', q * scale, k * scale)
        weight = jax.nn.softmax(weight, axis=-1)
        return jnp.einsum('bts,bcs->bct', weight, v)

    def _L0_attn_ref(hidden_states, Wq, Wk, Wv, Wo):
        import jax, jax.numpy as jnp
        import numpy as np
        NUM_HEADS = 8
        NUM_KV_HEADS = 2
        HEAD_DIM = 64
        HIDDEN = 512
        ROPE_THETA = 10000.0
        QUERY_PRE_ATTN_SCALAR = 256.0
        SOFTCAP = 50.0

        def _rope_cos_sin(S, dtype):
            inv_freq = 1.0 / ROPE_THETA ** (jnp.arange(0, HEAD_DIM, 2, dtype=jnp.float32) / HEAD_DIM)
            pos = jnp.arange(S, dtype=jnp.float32)
            freqs = pos[:, None] * inv_freq[None, :]
            emb = jnp.concatenate([freqs, freqs], axis=-1)
            return (jnp.cos(emb).astype(dtype), jnp.sin(emb).astype(dtype))

        def _rotate_half(x):
            x1, x2 = (x[..., :HEAD_DIM // 2], x[..., HEAD_DIM // 2:])
            return jnp.concatenate([-x2, x1], axis=-1)
        B, S, _ = hidden_states.shape
        q = jnp.einsum('bsh,dh->bsd', hidden_states, Wq).reshape(B, S, NUM_HEADS, HEAD_DIM).transpose(0, 2, 1, 3)
        k = jnp.einsum('bsh,dh->bsd', hidden_states, Wk).reshape(B, S, NUM_KV_HEADS, HEAD_DIM).transpose(0, 2, 1, 3)
        v = jnp.einsum('bsh,dh->bsd', hidden_states, Wv).reshape(B, S, NUM_KV_HEADS, HEAD_DIM).transpose(0, 2, 1, 3)
        cos, sin = _rope_cos_sin(S, hidden_states.dtype)
        cos = cos[None, None]
        sin = sin[None, None]
        q = q * cos + _rotate_half(q) * sin
        k = k * cos + _rotate_half(k) * sin
        groups = NUM_HEADS // NUM_KV_HEADS
        k = jnp.repeat(k, groups, axis=1)
        v = jnp.repeat(v, groups, axis=1)
        scale = QUERY_PRE_ATTN_SCALAR ** (-0.5)
        scores = jnp.einsum('bhqd,bhkd->bhqk', q, k) * scale
        scores = jnp.tanh(scores / SOFTCAP) * SOFTCAP
        probs = jax.nn.softmax(scores, axis=-1)
        attn = jnp.einsum('bhqk,bhkd->bhqd', probs, v)
        attn = attn.transpose(0, 2, 1, 3).reshape(B, S, NUM_HEADS * HEAD_DIM)
        return jnp.einsum('bsd,hd->bsh', attn, Wo)

    def _L0_ffn_ref(x, gate_w, w1, w2, w3, sw1, sw2, sw3, expert_bias):
        import jax, jax.numpy as jnp
        import numpy as np
        BS, SLEN, DIM, HID, E, TOPK = (4, 512, 512, 448, 8, 2)
        bs, slen, dim = x.shape
        T = bs * slen
        xf = x.reshape(T, dim)
        scores = jax.nn.softmax((xf @ gate_w).astype(jnp.float32), axis=-1)
        _, sel = jax.lax.top_k(scores + expert_bias[None, :], TOPK)
        top_scores = jnp.take_along_axis(scores, sel, axis=1)
        flat_sel = sel.reshape(-1)
        counts = jnp.bincount(flat_sel, length=E).astype(jnp.int32)
        order = jnp.argsort(flat_sel, stable=True)
        top_scores_sorted = top_scores.reshape(-1)[order]
        token_idx = order // TOPK
        routed_in = xf[token_idx] * top_scores_sorted[:, None]
        h = jax.nn.silu(jax.lax.ragged_dot(routed_in, w1, counts)) * jax.lax.ragged_dot(routed_in, w3, counts)
        routed_out = jax.lax.ragged_dot(h, w2, counts)
        out = jax.nn.silu(xf @ sw1) * (xf @ sw3) @ sw2
        out = out.at[token_idx].add(routed_out)
        return out.reshape(bs, slen, dim)
    h = _L0_tok_ref(x)
    h = h + _L0_attn_ref(_layernorm(h, axis=-1), L0_attn_Wq, L0_attn_Wk, L0_attn_Wv, L0_attn_Wo)
    h = h + _L0_ffn_ref(_layernorm(h, axis=-1), L0_ffn_gate_w, L0_ffn_w1, L0_ffn_w2, L0_ffn_w3, L0_ffn_sw1, L0_ffn_sw2, L0_ffn_sw3, L0_ffn_expert_bias)
    return h

_drawn_inputs = setup_inputs


def setup_inputs(seed=0):
    import zlib

    import numpy as np

    out = dict(_drawn_inputs(seed))
    spreads = {'L0_ffn_expert_bias': (0.0, 1.012)}
    factors = {'L0_ffn_gate_w': 4.595, 'L0_ffn_w1': 3.127, 'L0_ffn_w2': 3.114, 'L0_ffn_w3': 3.118}
    for name, (base, spread) in spreads.items():
        noise = np.random.default_rng([zlib.crc32(name.encode()), seed]).standard_normal(out[name].shape)
        drawn = base * np.exp(spread * noise) if base else spread * noise
        out[name] = jnp.asarray(drawn.astype(out[name].dtype))
    for name, factor in factors.items():
        out[name] = (out[name] * factor).astype(out[name].dtype)
    return out
```

```python
from contextlib import ExitStack

import concourse.bass as bass
from concourse import mybir

F32 = mybir.dt.float32
F32R = mybir.dt.float32r
BF16 = mybir.dt.bfloat16
I32 = mybir.dt.int32
U32 = mybir.dt.uint32
ALU = mybir.AluOpType
ACT = mybir.ActivationFunctionType
AX = mybir.AxisListType

P = 128
EPS = 1e-5
GROUP_TILES = 4
GROUP = GROUP_TILES * P


class Signal:

    def __init__(self, sem, per=1, batches=None):
        self.sem, self.per, self.batches = sem, per, batches

    def at(self, batch, k=None):
        j, off = batch
        if self.batches and isinstance(j, int) and 2 * j + off >= self.batches:
            j, off, k = 0, self.batches - 1, None
        value = 2 * self.per * j + (self.per * off + (self.per if k is None else k))
        return max(value, 0) if isinstance(value, int) else value


class DmaSignal:

    def __init__(self, even, odd, per=1):
        self.sems, self.per = (even, odd), per

    def of(self, batch):
        return self.sems[batch[1] % 2]

    def at(self, batch):
        value = 16 * self.per * batch[0] + 16 * self.per * (batch[1] // 2 + 1)
        return max(value, 0) if isinstance(value, int) else value


def back(batch, k):
    return (batch[0], batch[1] - k)


def audio_tower(nc, x, wq, wk, wv, wo, gate_w, w1, w2, w3, sw1, sw2, sw3, expert_bias, cos, sin, out):
    NB, C3, D = x.shape
    C = C3 // 3
    E, _, HID = w1.shape
    HD = 64
    NH = wq.shape[0] // HD
    NKV = wk.shape[0] // HD
    G = NH // NKV
    QKV = (NH + 2 * NKV) * HD
    QK = (NH + NKV) * HD
    KC = D // P
    HC = 4
    HW = HID // HC
    HG = HID + E
    TOKENS = NB * C
    CAP = -(-TOKENS // GROUP) * GROUP + GROUP
    ENTRY = 2
    NOWHERE = 1 << 22
    NG = (2 * TOKENS - E) // GROUP + E
    NG += NG % 2
    STEPS_IN, STEPS_OUT = 6, 5
    LAG = 3
    assert NB % 2 == 0 and D == 512 and HW * HC == HID and NH == 8 and NKV == 2

    REGIONS = -(-(E * CAP + GROUP) // P) * P
    routed = nc.dram_tensor("routed_entries", (REGIONS, ENTRY), F32).ap()
    normed = nc.dram_tensor("normed_rows", (TOKENS, D), F32).ap()

    with ExitStack() as ctx:
        def sem(name):
            return ctx.enter_context(nc.semaphore(name))

        def sbuf(name, shape, dt=F32, where=ctx):
            return where.enter_context(nc.sbuf_tensor(name, shape, dt))

        def signal(name, per=1):
            return Signal(sem(name), per, NB)

        def dma_signal(name, per=1):
            return DmaSignal(sem(name + "_even"), sem(name + "_odd"), per)

        ps = ctx.enter_context(nc.psum_tensor("ps", [P, 8, 512], F32))
        ident = sbuf("ident", [P, P])
        ones = sbuf("ones", [P, P])
        base = sbuf("base", [P, E])

        tower = ctx.enter_context(ExitStack())

        def resident(name, shape):
            return (sbuf(name + "_hi", shape, F32R, tower), sbuf(name + "_lo", shape, F32R, tower))

        wqkv = resident("wqkv", [P, KC, QKV])
        woT = resident("woT", [P, KC, D])
        w1g = resident("w1g", [P, KC, HG])
        w3s = resident("w3s", [P, KC, HID])
        w2s = resident("w2s", [HW, HC, D])
        cos_t = sbuf("cos_t", [P, HD], F32, tower)
        sin_t = sbuf("sin_t", [P, HD], F32, tower)
        bias_t = sbuf("bias_t", [P, E], F32, tower)
        iota8 = sbuf("iota8", [P, E], F32, tower)
        tri = sbuf("tri", [P, P], BF16, tower)
        ones16 = sbuf("ones16", [P, P], BF16, tower)
        mhalf = sbuf("mhalf", [P, 1], F32, tower)
        tokf = sbuf("tokf", [P, 1], F32, tower)
        X = [sbuf(f"X{p}", [P, 3, D], F32, tower) for p in range(2)]
        vaug = [sbuf(f"vaug{p}", [P, NKV, HD + 1], F32, tower) for p in range(2)]
        vT = [sbuf(f"vT{p}", [P, KC, C + 1], F32, tower) for p in range(2)]

        with ExitStack() as c0:
            s_raw, s_const, s_const2, s_pe, s_hi, s_lo, s_set, s_empty = (
                c0.enter_context(nc.semaphore(n)) for n in
                ("s_raw", "s_const", "s_const2", "s_pe", "s_hi", "s_lo", "s_set", "s_empty"))
            raw_q = sbuf("raw_q", [P, KC, D], F32, c0)
            raw_k = sbuf("raw_k", [P, D], F32, c0)
            raw_v = sbuf("raw_v", [P, D], F32, c0)
            raw_o = sbuf("raw_o", [P, KC, D], F32, c0)
            raw_1 = sbuf("raw_1", [P, KC, HG], F32, c0)
            raw_3 = sbuf("raw_3", [P, KC, HID], F32, c0)
            raw_2 = sbuf("raw_2", [HW, HC, D], F32, c0)
            trif = sbuf("trif", [P, P], F32, c0)
            empty = sbuf("empty", [P, REGIONS // P, ENTRY], F32, c0)
            n_loads = [0]
            N_LOADS = NH + 11
            jobs = [(raw_q[:, j, :], wqkv, P * j) for j in range(KC)]
            jobs += [(raw_k[:, :], wqkv, NH * HD), (raw_v[:, :], wqkv, QK)]
            jobs += [(raw_o[:, j, :], woT, P * j) for j in range(KC)]
            direct = [(raw_1, w1g), (raw_3, w3s), (raw_2, w2s)]

            with nc.Block() as block:
                @block.sync
                def _(sp):
                    def load(dst, src):
                        sp.dma_start(dst, src).then_inc(s_raw, 16)
                        n_loads[0] += 1
                    for j in range(G):
                        for g in range(NKV):
                            load(raw_q[g * HD:(g + 1) * HD, j, :], wq[(g * G + j) * HD:(g * G + j + 1) * HD, :])
                    load(raw_k[:, :], wk)
                    load(raw_v[:, :], wv)
                    load(raw_o[:, :, :], wo.rearrange("(j p) d -> p j d", p=P))
                    load(raw_1[:, :, 0:HID], sw1.rearrange("(k p) h -> p k h", p=P))
                    load(raw_1[:, :, HID:HG], gate_w.rearrange("(k p) h -> p k h", p=P))
                    load(raw_3[:, :, :], sw3.rearrange("(k p) h -> p k h", p=P))
                    load(raw_2[:, :, :], sw2.rearrange("(k p) h -> p k h", p=HW))
                    load(cos_t[0:C, :], cos)
                    load(sin_t[0:C, :], sin)
                    sp.wait_ge(s_empty, 2)
                    load(routed.rearrange("(p n) c -> p n c", p=P), empty[:, :, :])
                    load(bias_t[:, :], expert_bias.rearrange("(o e) -> o e", o=1).to_broadcast([P, E]))
                    assert n_loads[0] == N_LOADS
                    sp.wait_ge(s_raw, 16 * N_LOADS)

                @block.gpsimd
                def _(pool):
                    nc.gpsimd.memset(ident[:], 0.0).then_inc(s_const, 1)
                    nc.gpsimd.memset(trif[:], 1.0).then_inc(s_const, 1)
                    nc.gpsimd.iota(iota8[:], [[1, E]], base=0, channel_multiplier=0,
                                   allow_small_or_imprecise_dtypes=True).then_inc(s_const, 1)
                    nc.gpsimd.iota(base[:], [[CAP, E]], base=0, channel_multiplier=0,
                                   allow_small_or_imprecise_dtypes=True).then_inc(s_const, 1)
                    nc.gpsimd.iota(tokf[:], [[1, 1]], base=-C, channel_multiplier=1,
                                   allow_small_or_imprecise_dtypes=True).then_inc(s_const, 1)
                    pool.wait_ge(s_const, 5)
                    nc.gpsimd.affine_select(out=ident[:], in_=ident[:], compare_op=ALU.not_equal, fill=1.0,
                                            base=0, pattern=[[-1, P]], channel_multiplier=1).then_inc(s_const2, 1)
                    nc.gpsimd.affine_select(out=trif[:], in_=trif[:], compare_op=ALU.is_gt, fill=0.0,
                                            base=0, pattern=[[1, P]], channel_multiplier=-1).then_inc(s_const2, 1)

                @block.vector
                def _(dve):
                    nc.vector.memset(empty[:, :, 0].bitcast(I32), NOWHERE).then_inc(s_empty, 1)
                    nc.vector.memset(empty[:, :, 1], 0.0).then_inc(s_empty, 1)
                    nc.vector.memset(ones[:], 1.0).then_inc(s_set, 1)
                    nc.vector.memset(ones16[:], 1.0).then_inc(s_set, 1)
                    nc.vector.memset(mhalf[:], -0.5).then_inc(s_set, 1)
                    for p in range(2):
                        nc.vector.memset(X[p][96:P, 1, :], 1.0).then_inc(s_set, 1)
                        nc.vector.memset(vaug[p][:, :, HD:HD + 1], 1.0).then_inc(s_set, 1)
                        nc.vector.memset(vT[p][:, :, C:C + 1], 1.0).then_inc(s_set, 1)
                    dve.wait_ge(s_const2, 2)
                    nc.vector.tensor_copy(tri[:], trif[:]).then_inc(s_set, 1)
                    for n, (_, w, col) in enumerate(jobs):
                        dve.wait_ge(s_hi, n + 1)
                        nc.vector.tensor_tensor(w[1][:, :, col:col + P],
                                                ps[:, n % 2, :].rearrange("p (k m) -> p k m", k=KC),
                                                w[0][:, :, col:col + P].bitcast(F32), ALU.subtract).then_inc(s_lo, 1)
                    for n, (raw, w) in enumerate(direct):
                        dve.wait_ge(s_hi, len(jobs) + n + 1)
                        nc.vector.tensor_tensor(w[1][:], raw[:], w[0][:].bitcast(F32), ALU.subtract).then_inc(s_lo, 1)

                @block.tensor
                def _(pe):
                    pe.wait_ge(s_raw, 16 * N_LOADS)
                    pe.wait_ge(s_const2, 2)
                    for n, (src, _, _) in enumerate(jobs):
                        if n >= 2:
                            pe.wait_ge(s_lo, n - 1)
                        for k in range(KC):
                            last = nc.tensor.transpose(ps[:, n % 2, k * P:(k + 1) * P], src[:, k * P:(k + 1) * P],
                                                       ident[:])
                        last.then_inc(s_pe, 1)

                @block.scalar
                def _(act):
                    for n, (_, w, col) in enumerate(jobs):
                        act.wait_ge(s_pe, n + 1)
                        nc.scalar.activation(w[0][:, :, col:col + P],
                                             ps[:, n % 2, :].rearrange("p (k m) -> p k m", k=KC),
                                             ACT.Copy).then_inc(s_hi, 1)
                    act.wait_ge(s_raw, 16 * N_LOADS)
                    for raw, w in direct:
                        nc.scalar.activation(w[0][:], raw[:], ACT.Copy).then_inc(s_hi, 1)

        def pair(name, shape, dt=F32):
            return [sbuf(f"{name}{p}", shape, dt, tower) for p in range(2)]

        def one(name, shape, dt=F32):
            return sbuf(name, shape, dt, tower)

        qk_r = pair("qk_r", [P, 2, D], F32R)
        negmax = pair("negmax", [P, KC])
        mrow = pair("mrow", [KC, P])
        e = one("e", [P, KC, D])
        hz = one("hz", [P, D])
        rz = one("rz", [P, KC])
        diag = one("diag", [P, KC, P])
        h = pair("h", [P, D])
        st1, ag1 = one("st1", [P, 6]), one("ag1", [P, 2])
        st2, ag2 = one("st2", [P, 6]), one("ag2", [P, 2])
        ve1, rs1 = one("ve1", [P, 1]), one("rs1", [P, 1])
        ve2, rs2 = one("ve2", [P, 1]), one("rs2", [P, 1])
        xn = one("xn", [P, D])
        xT = (one("xT_hi", [P, KC, P], F32R), one("xT_lo", [P, KC, P], F32R))
        rc = one("rc", [P, QK])
        rsn = one("rsn", [P, QK])
        qkr = one("qkr", [P, QK])
        qkT = one("qkT", [P, NH // 2 + 1, C])
        pT = one("pT", [P, NKV, G * C])
        rden = one("rden", [P, NH])
        attn = one("attn", [P, NH, HD])
        aT = (one("aT_hi", [P, KC, P], F32R), one("aT_lo", [P, KC, P], F32R))
        h2 = pair("h2", [P, D])
        y = pair("y", [P, D])
        yT = (one("yT_hi", [P, KC, P], F32R), one("yT_lo", [P, KC, P], F32R))
        th = one("th", [P, HID])
        ga = one("ga", [P, HID])
        gb = one("gb", [P, HID])
        hT = (one("hT_hi", [P, HC, P], F32R), one("hT_lo", [P, HC, P], F32R))
        h3 = pair("h3", [P, D])
        nl, ex, se, rse = one("nl", [P, 1]), one("ex", [P, E]), one("se", [P, 1]), one("rse", [P, 1])
        sc, met, v8, i8 = one("sc", [P, E]), one("met", [P, E]), one("v8", [P, E]), one("i8", [P, E], U32)
        i2 = one("i2", [P, 2])
        oh = one("oh", [P, 2, E])
        m16 = one("m16", [P, E], BF16)
        junk = one("junk", [P, E])
        posb = one("posb", [P, E])
        slotf = one("slotf", [P, 2])
        slot = pair("slot", [P, 2], I32)
        entry = [pair(f"entry{k}_", [P, ENTRY]) for k in range(2)]

        x_in = dma_signal("x_in")
        row_in = dma_signal("row_in")
        h3_out = dma_signal("h3_out")
        y_out = dma_signal("y_out")
        scattered = dma_signal("scattered", 2)
        xT_ps, vT_ps, mx_ps = signal("xT_ps"), signal("vT_ps"), signal("mx_ps", KC)
        qkv_ps, mt_ps, yT_ps, up_ps = signal("qkv_ps"), signal("mt_ps"), signal("yT_ps"), signal("up_ps")
        qk_ps, rT_ps, hT_ps, dn_ps = signal("qk_ps", KC), signal("rT_ps"), signal("hT_ps"), signal("dn_ps")
        s_ps, o_ps, pv_ps, zt_ps = signal("s_ps", 2), signal("o_ps"), signal("pv_ps"), signal("zt_ps")
        rank_ps, aT_ps, bc_ps, wo_ps = signal("rank_ps"), signal("aT_ps"), signal("bc_ps"), signal("wo_ps")
        xT_hi, vT_sb, yT_hi, v_sb, th_sb = (signal(n) for n in ("s_xT_hi", "vT_sb", "s_yT_hi", "v_sb", "th_sb"))
        ex_sb, e_sb, qkT_sb, hT_hi = signal("ex_sb"), signal("e_sb", KC), signal("qkT_sb"), signal("s_hT_hi")
        tanh_sb, p_sb, hz_sb, aT_hi = signal("tanh_sb", 2), signal("p_sb", 2), signal("hz_sb"), signal("s_aT_hi")
        xT_lo, max_sb, mrow_sb, yT_lo = signal("s_xT_lo"), signal("max_sb", KC), signal("mrow_sb"), signal("s_yT_lo")
        rope_sb, nl_sb, ga_sb, gb_sb = signal("rope_sb", 3), signal("nl_sb"), signal("ga_sb"), signal("gb_sb")
        hT_lo, h3_sb, pick, m16_sb = signal("s_hT_lo"), signal("h3_sb"), signal("pick", 12), signal("m16_sb")
        rden_sb, attn_sb, rz_sb, diag_sb = signal("rden_sb"), signal("attn_sb"), signal("rz_sb"), signal("diag_sb")
        place, aT_lo, h_sb = signal("place", 5), signal("s_aT_lo"), signal("h_sb")
        st1_sb, ag1_sb, xn_sb = signal("st1_sb"), signal("ag1_sb"), signal("xn_sb")
        h2_sb, st2_sb, ag2_sb, y_sb = signal("h2_sb"), signal("st2_sb"), signal("ag2_sb"), signal("y_sb")
        qkr_r, rope_add, ve1_sb, rs1_sb = signal("qkr_r"), signal("rope_add"), signal("ve1_sb"), signal("rs1_sb")
        ve2_sb, rs2_sb = signal("ve2_sb"), signal("rs2_sb")
        past = sem("past")

        def alone(eng):
            eng.sem_inc(past, 1)

        def split_matmuls(dst, lhs, rhs, chunks, first, last_chunk, rows, cols):
            ins = None
            for k in chunks:
                for i, (a, b) in enumerate(((0, 0), (1, 0), (0, 1))):
                    ins = nc.tensor.matmul(dst, lhs[a][:rows, k, 0:C], rhs[b][:rows, k, cols[0]:cols[1]],
                                           start=(k == first and i == 0), stop=(k == last_chunk and i == 2))
            return ins

        def each_step(eng, step):
            def static(n):
                step((0, n), lambda lag: 0 <= n - lag < NB, n)
            for n in range(STEPS_IN):
                static(n)
            with eng.Fori(STEPS_IN // 2, (NB - 2) // 2) as j:
                for p in range(2):
                    step((j, p), lambda lag: True, None)
            for n in range(NB - 2, NB + LAG):
                static(n)

        QS = 1.0 / float(C) ** 0.5
        CAPF = 50.0
        TANH = 1.0 / (16.0 * CAPF)

        with nc.Block() as block:
            @block.sync
            def _(sp):
                def load(b):
                    sp.wait_ge(qk_ps.sem, qk_ps.at(back(b, 2)))
                    alone(sp)
                    p = b[1] % 2
                    src = x[b[1]] if isinstance(b[0], int) and b[0] == 0 else \
                        x[bass.ds(2 * b[0] + b[1], 1)].rearrange("o c d -> (o c) d")
                    sp.dma_start(X[p][0:C, :, :], src.rearrange("(a c) d -> c a d", a=3)).then_inc(x_in.of(b), 16)

                def step(t, has, n):
                    if n == 0:
                        load(t)
                    if has(-1):
                        load(back(t, -1))
                    if has(0):
                        sp.wait_ge(mrow_sb.sem, mrow_sb.at(t))
                        sp.dma_start(X[t[1] % 2][C:C + 1, 0, :].rearrange("o (a b) -> o a b", a=KC),
                                                 mrow[t[1] % 2][:, :]).then_inc(row_in.of(t), 16)
                    if has(2):
                        f = back(t, 2)
                        sp.wait_ge(y_sb.sem, y_sb.at(f))
                        alone(sp)
                        row0 = C * (2 * f[0] + f[1])
                        dst = normed[row0:row0 + C, :] if isinstance(row0, int) else normed[bass.ds(row0, C), :]
                        sp.dma_start(dst, y[f[1] % 2][0:C, :]).then_inc(y_out.of(f), 16)
                        sp.wait_ge(h3_sb.sem, h3_sb.at(f))
                        alone(sp)
                        row0 = C * (2 * f[0] + f[1])
                        dst = out[row0:row0 + C, :] if isinstance(row0, int) else out[bass.ds(row0, C), :]
                        sp.dma_start(dst, h3[f[1] % 2][0:C, :]).then_inc(h3_out.of(f), 16)
                each_step(sp, step)
                for b in ((0, NB - 2), (0, NB - 1)):
                    sp.wait_ge(h3_out.of(b), h3_out.at(b))
                    sp.wait_ge(y_out.of(b), y_out.at(b))

            @block.tensor
            def _(pe):
                def step(t, has, n):
                    a, f = back(t, 1), back(t, 2)
                    p = t[1] % 2
                    if has(1):
                        pe.wait_ge(xn_sb.sem, xn_sb.at(a))
                        pe.wait_ge(attn_sb.sem, attn_sb.at(back(a, 1)))
                        for k in range(KC):
                            last = nc.tensor.transpose(ps[:, 3, k * C:(k + 1) * C], xn[0:C, k * P:(k + 1) * P],
                                                       ident[0:C, 0:C])
                        last.then_inc(xT_ps.sem, 1)
                    if has(0):
                        pe.wait_ge(x_in.of(t), x_in.at(t))
                        pe.wait_ge(attn_sb.sem, attn_sb.at(back(a, 1)))
                        for k in range(KC):
                            last = nc.tensor.transpose(ps[:, 2, k * C:(k + 1) * C],
                                                       X[p][0:C, 2, k * P:(k + 1) * P], ident[0:C, 0:C])
                        last.then_inc(vT_ps.sem, 1)
                        pe.wait_ge(qkr_r.sem, qkr_r.at(t))
                        pe.wait_ge(hz_sb.sem, hz_sb.at(back(t, 1)))
                        pe.wait_ge(place.sem, place.at(back(f, 1)))
                        for i in range(KC):
                            if i >= 2:
                                pe.wait_ge(max_sb.sem, max_sb.at(t, i - 1))
                            nc.tensor.matmul(ps[:, i % 2, :], qk_r[p][0:C, 0, i * P:(i + 1) * P],
                                                        qk_r[p][0:C, 1, :], start=True, stop=True).then_inc(mx_ps.sem, 1)
                    if has(1):
                        pe.wait_ge(xT_lo.sem, xT_lo.at(a))
                        pe.wait_ge(rz_sb.sem, rz_sb.at(back(t, 1)))
                        pe.wait_ge(aT_lo.sem, aT_lo.at(back(a, 1)))
                        split_matmuls(ps[0:C, 4, :], xT, wqkv, range(KC), 0, KC - 1, P, (0, D))
                        split_matmuls(ps[0:C, 5, 0:QKV - D], xT, wqkv, range(KC), 0, KC - 1, P, (D, QKV)).then_inc(qkv_ps.sem, 1)
                    if has(0):
                        pe.wait_ge(max_sb.sem, max_sb.at(t))
                        pe.wait_ge(vT_sb.sem, vT_sb.at(t))
                        nc.tensor.transpose(ps[0:KC, 2, 0:P], negmax[p][:, :], ident[:, :]).then_inc(mt_ps.sem, 1)
                    if has(2):
                        pe.wait_ge(y_sb.sem, y_sb.at(f))
                        if has(1):
                            pe.wait_ge(xT_lo.sem, xT_lo.at(a))
                        for k in range(KC):
                            last = nc.tensor.transpose(ps[:, 3, k * C:(k + 1) * C], y[p][0:C, k * P:(k + 1) * P],
                                                       ident[0:C, 0:C])
                        last.then_inc(yT_ps.sem, 1)
                        pe.wait_ge(yT_lo.sem, yT_lo.at(f))
                        pe.wait_ge(h2_sb.sem, h2_sb.at(back(a, 1)))
                        pe.wait_ge(h_sb.sem, h_sb.at(back(t, 1)))
                        split_matmuls(ps[0:C, 6, 0:HG], yT, w1g, range(KC), 0, KC - 1, P, (0, HG))
                        split_matmuls(ps[0:C, 7, 0:HID], yT, w3s, range(KC), 0, KC - 1, P, (0, HID)).then_inc(up_ps.sem, 1)
                    if has(0):
                        pe.wait_ge(row_in.of(t), row_in.at(t))
                        for i in range(KC):
                            if i >= 2:
                                pe.wait_ge(e_sb.sem, e_sb.at(t, i - 1))
                            else:
                                pe.wait_ge(max_sb.sem, max_sb.at(t))
                            nc.tensor.matmul(ps[:, i % 2, :], X[p][0:C + 1, 1, i * P:(i + 1) * P],
                                                        X[p][0:C + 1, 0, :], start=True, stop=True).then_inc(qk_ps.sem, 1)
                    if has(1):
                        pe.wait_ge(rope_add.sem, rope_add.at(a))
                        if has(0):
                            pe.wait_ge(mrow_sb.sem, mrow_sb.at(t))
                        if has(2):
                            pe.wait_ge(yT_lo.sem, yT_lo.at(f))
                        for k in range(NH // 2 + 1):
                            last = nc.tensor.transpose(ps[:, 2 + k // 4, (k % 4) * C:(k % 4 + 1) * C],
                                                       qkr[0:C, k * P:(k + 1) * P], ident[0:C, 0:C])
                        last.then_inc(rT_ps.sem, 1)
                    if has(2):
                        pe.wait_ge(gb_sb.sem, gb_sb.at(f))
                        if has(1):
                            pe.wait_ge(rope_sb.sem, rope_sb.at(a))
                        for k in range(HC):
                            last = nc.tensor.transpose(ps[0:HW, 4, k * C:(k + 1) * C],
                                                       gb[0:C, k * HW:(k + 1) * HW], ident[0:C, 0:C])
                        last.then_inc(hT_ps.sem, 1)
                        pe.wait_ge(hT_lo.sem, hT_lo.at(f))
                        pe.wait_ge(ga_sb.sem, ga_sb.at(f))
                        pe.wait_ge(ex_sb.sem, ex_sb.at(f))
                        split_matmuls(ps[0:C, 6, :], hT, w2s, range(HC), 0, HC - 1, HW, (0, D)).then_inc(dn_ps.sem, 1)
                    if has(1):
                        pe.wait_ge(qkT_sb.sem, qkT_sb.at(a))
                        pe.wait_ge(v_sb.sem, v_sb.at(a))
                        pe.wait_ge(rope_sb.sem, rope_sb.at(a))
                        if has(2):
                            pe.wait_ge(gb_sb.sem, gb_sb.at(f))
                        for g in range(NKV):
                            r = slice(g * HD, (g + 1) * HD)
                            nc.tensor.matmul(ps[0:C, 5 + 2 * g, 0:G * C], qkT[r, NH // 2, :],
                                                       qkT[r, 0:G, :].rearrange("p a b -> p (a b)"),
                                                       start=True, stop=True).then_inc(s_ps.sem, 1)
                    if has(0):
                        for i in range(KC):
                            pe.wait_ge(e_sb.sem, e_sb.at(t, max(i + 1, 3)))
                            last = nc.tensor.matmul(ps[0:C + 1, 0, :], vT[p][:, i, :], e[:, i, :],
                                                    start=(i == 0), stop=(i == KC - 1))
                        last.then_inc(o_ps.sem, 1)
                    if has(1):
                        pe.wait_ge(qkT_sb.sem, qkT_sb.at(a))
                        for g in range(NKV):
                            pe.wait_ge(p_sb.sem, p_sb.at(a, g + 1))
                            for j in range(G):
                                last = nc.tensor.matmul(ps[0:C, 2 + g, j * (HD + 1):(j + 1) * (HD + 1)],
                                                        pT[0:C, g, j * C:(j + 1) * C], vaug[a[1] % 2][0:C, g, :],
                                                        start=True, stop=True)
                        last.then_inc(pv_ps.sem, 1)
                    if has(0):
                        pe.wait_ge(hz_sb.sem, hz_sb.at(t))
                        if has(2):
                            pe.wait_ge(hT_lo.sem, hT_lo.at(f))
                        w = C + 1 - 96
                        alone(pe)
                        for i in range(KC):
                            last = nc.tensor.transpose(ps[:, 4, i * w:(i + 1) * w], hz[96:C + 1, i * P:(i + 1) * P],
                                                       ident[96:C + 1, 96:C + 1])
                        last.then_inc(zt_ps.sem, 1)
                    if has(2):
                        pe.wait_ge(m16_sb.sem, m16_sb.at(f))
                        if has(0):
                            pe.wait_ge(e_sb.sem, e_sb.at(t))
                        nc.tensor.matmul(ps[0:C, 1, 0:E], tri[0:C, 0:C], m16[0:C, :], start=True, stop=True)
                        nc.tensor.matmul(ps[:, 1, E:2 * E], ones16[0:C, :], m16[0:C, :],
                                                      start=True, stop=True).then_inc(rank_ps.sem, 1)
                    if has(1):
                        pe.wait_ge(attn_sb.sem, attn_sb.at(a))
                        pe.wait_ge(tanh_sb.sem, tanh_sb.at(a))
                        for k in range(KC):
                            last = nc.tensor.transpose(ps[:, 5, k * C:(k + 1) * C],
                                                       attn[0:C, 2 * k:2 * k + 2, :].rearrange("p a b -> p (a b)"),
                                                       ident[0:C, 0:C])
                        last.then_inc(aT_ps.sem, 1)
                    if has(0):
                        pe.wait_ge(diag_sb.sem, diag_sb.at(t))
                        if has(1):
                            pe.wait_ge(tanh_sb.sem, tanh_sb.at(a))
                        for i in range(KC):
                            last = nc.tensor.matmul(ps[0:C, 7, i * P:(i + 1) * P], ones[:, 0:C], diag[:, i, :],
                                                    start=True, stop=True)
                        last.then_inc(bc_ps.sem, 1)
                    if has(1):
                        pe.wait_ge(aT_lo.sem, aT_lo.at(a))
                        if has(2):
                            pe.wait_ge(h3_sb.sem, h3_sb.at(f))
                        split_matmuls(ps[0:C, 6, :], aT, woT, range(KC), 0, KC - 1, P, (0, D)).then_inc(wo_ps.sem, 1)
                each_step(pe, step)

            @block.scalar
            def _(act):
                def hi_part(dst, bank, rows):
                    return nc.scalar.activation(dst[0][0:rows, :, 0:C],
                                                ps[0:rows, bank, 0:KC * C].rearrange("p (k c) -> p k c", k=KC), ACT.Copy)

                def step(t, has, n):
                    a, f = back(t, 1), back(t, 2)
                    p = t[1] % 2
                    if has(1):
                        act.wait_ge(xT_ps.sem, xT_ps.at(a))
                        act.wait_ge(qkv_ps.sem, qkv_ps.at(back(a, 1)))
                        hi_part(xT, 3, P).then_inc(xT_hi.sem, 1)
                    if has(0):
                        act.wait_ge(vT_ps.sem, vT_ps.at(t))
                        act.wait_ge(o_ps.sem, o_ps.at(back(t, 2)))
                        nc.scalar.activation(
                            vT[p][:, :, 0:C], ps[:, 2, 0:KC * C].rearrange("p (k c) -> p k c", k=KC), ACT.Copy).then_inc(vT_sb.sem, 1)
                    if has(1):
                        act.wait_ge(qkv_ps.sem, qkv_ps.at(a))
                        act.wait_ge(pv_ps.sem, pv_ps.at(back(a, 2)))
                        nc.scalar.activation(
                            vaug[a[1] % 2][0:C, :, 0:HD],
                            ps[0:C, 5, QK - D:QKV - D].rearrange("p (g d) -> p g d", g=NKV), ACT.Copy).then_inc(v_sb.sem, 1)
                    if has(2):
                        act.wait_ge(yT_ps.sem, yT_ps.at(f))
                        act.wait_ge(up_ps.sem, up_ps.at(back(f, 1)))
                        hi_part(yT, 3, P).then_inc(yT_hi.sem, 1)
                        act.wait_ge(up_ps.sem, up_ps.at(f))
                        act.wait_ge(ga_sb.sem, ga_sb.at(back(f, 1)))
                        nc.scalar.activation(th[0:C, :], ps[0:C, 6, 0:HID], ACT.Tanh, scale=0.5).then_inc(th_sb.sem, 1)
                        act.wait_ge(nl_sb.sem, nl_sb.at(f))
                        act.wait_ge(pick.sem, pick.at(back(f, 1)))
                        nc.scalar.activation(ex[0:C, :], ps[0:C, 6, HID:HG], ACT.Exp, bias=nl[0:C, :],
                                                        accum_out=se[0:C, :]).then_inc(ex_sb.sem, 1)
                    if has(0):
                        for i in range(KC):
                            act.wait_ge(qk_ps.sem, qk_ps.at(t, i + 1))
                            if i == 0:
                                act.wait_ge(o_ps.sem, o_ps.at(back(t, 1)))
                            nc.scalar.activation(e[:, i, :], ps[:, i % 2, :], ACT.Exp, scale=QS).then_inc(e_sb.sem, 1)
                    if has(1):
                        act.wait_ge(rT_ps.sem, rT_ps.at(a))
                        act.wait_ge(s_ps.sem, s_ps.at(back(a, 1)))
                        nc.scalar.activation(qkT[:, 0:4, :], ps[:, 2, 0:4 * C].rearrange("p (k c) -> p k c", k=4), ACT.Copy)
                        nc.scalar.activation(qkT[:, 4, :], ps[:, 3, 0:C], ACT.Copy).then_inc(qkT_sb.sem, 1)
                    if has(2):
                        act.wait_ge(hT_ps.sem, hT_ps.at(f))
                        act.wait_ge(dn_ps.sem, dn_ps.at(back(f, 1)))
                        hi_part(hT, 4, HW).then_inc(hT_hi.sem, 1)
                    if has(1):
                        for g in range(NKV):
                            act.wait_ge(s_ps.sem, s_ps.at(a, g + 1))
                            if g == 0:
                                act.wait_ge(pv_ps.sem, pv_ps.at(back(a, 1)))
                            nc.scalar.activation(pT[0:C, g, :], ps[0:C, 5 + 2 * g, 0:G * C], ACT.Tanh,
                                                              scale=TANH).then_inc(tanh_sb.sem, 1)
                        for g in range(NKV):
                            act.wait_ge(tanh_sb.sem, tanh_sb.at(a, g + 1))
                            nc.scalar.activation(pT[0:C, g, :], pT[0:C, g, :], ACT.Exp, scale=CAPF).then_inc(p_sb.sem, 1)
                    if has(0):
                        act.wait_ge(o_ps.sem, o_ps.at(t))
                        act.wait_ge(zt_ps.sem, zt_ps.at(back(t, 1)))
                        act.wait_ge(h_sb.sem, h_sb.at(back(t, 1)))
                        nc.scalar.activation(hz[0:C + 1, :], ps[0:C + 1, 0, :], ACT.Copy).then_inc(hz_sb.sem, 1)
                    if has(1):
                        act.wait_ge(aT_ps.sem, aT_ps.at(a))
                        act.wait_ge(wo_ps.sem, wo_ps.at(back(a, 1)))
                        hi_part(aT, 5, P).then_inc(aT_hi.sem, 1)
                each_step(act, step)

            @block.vector
            def _(dve):
                def lo_part(dst, bank, rows):
                    return nc.vector.tensor_tensor(dst[1][0:rows, :, 0:C],
                                                   ps[0:rows, bank, 0:KC * C].rearrange("p (k c) -> p k c", k=KC),
                                                   dst[0][0:rows, :, 0:C].bitcast(F32), ALU.subtract)

                def step(t, has, n):
                    a, f = back(t, 1), back(t, 2)
                    p = t[1] % 2
                    pa = a[1] % 2
                    if has(1):
                        dve.wait_ge(xT_hi.sem, xT_hi.at(a))
                        dve.wait_ge(qkv_ps.sem, qkv_ps.at(back(a, 1)))
                        lo_part(xT, 3, P).then_inc(xT_lo.sem, 1)
                    if has(0):
                        for i in range(KC):
                            dve.wait_ge(mx_ps.sem, mx_ps.at(t, i + 1))
                            if i == 0:
                                dve.wait_ge(mt_ps.sem, mt_ps.at(back(t, 2)))
                            nc.vector.tensor_reduce(negmax[p][:, i:i + 1], ps[:, i % 2, :], AX.X, ALU.max,
                                                                negate=True).then_inc(max_sb.sem, 1)
                        dve.wait_ge(mt_ps.sem, mt_ps.at(t))
                        dve.wait_ge(row_in.of(back(t, 2)), row_in.at(back(t, 2)))
                        nc.vector.tensor_copy(mrow[p][:, :], ps[0:KC, 2, 0:P]).then_inc(mrow_sb.sem, 1)
                    if has(2):
                        dve.wait_ge(yT_hi.sem, yT_hi.at(f))
                        dve.wait_ge(up_ps.sem, up_ps.at(back(f, 1)))
                        lo_part(yT, 3, P).then_inc(yT_lo.sem, 1)
                    if has(1):
                        dve.wait_ge(v_sb.sem, v_sb.at(a))
                        dve.wait_ge(rope_add.sem, rope_add.at(back(a, 1)))
                        heads = QK // HD
                        src = ps[0:C, 4:6, :].rearrange("p a b -> p (a b)")[:, 0:QK].rearrange(
                            "p (h s d) -> p h s d", h=heads, s=2)
                        cb = cos_t[0:C, None, :].to_broadcast([C, heads, HD])
                        nc.vector.tensor_tensor(
                            rc[0:C, :].rearrange("p (h d) -> p h d", h=heads),
                            ps[0:C, 4:6, :].rearrange("p a b -> p (a b)")[:, 0:QK].rearrange("p (h d) -> p h d", h=heads),
                            cb, ALU.mult).then_inc(rope_sb.sem, 1)
                        dst = rsn[0:C, :].rearrange("p (h s d) -> p h s d", h=heads, s=2)
                        for s in range(2):
                            sb_ = sin_t[0:C, None, s * (HD // 2):(s + 1) * (HD // 2)].to_broadcast([C, heads, HD // 2])
                            nc.vector.tensor_tensor(dst[:, :, s, :], src[:, :, 1 - s, :], sb_, ALU.mult).then_inc(rope_sb.sem, 1)
                    if has(2):
                        dve.wait_ge(th_sb.sem, th_sb.at(f))
                        dve.wait_ge(pick.sem, pick.at(back(f, 1)))
                        nc.vector.tensor_reduce(nl[0:C, :], ps[0:C, 6, HID:HG], AX.X, ALU.max, negate=True).then_inc(nl_sb.sem, 1)
                        dve.wait_ge(ex_sb.sem, ex_sb.at(f))
                        nc.vector.scalar_tensor_tensor(ga[0:C, :], th[0:C, :], 1.0, ps[0:C, 6, 0:HID],
                                                                  ALU.add, ALU.mult).then_inc(ga_sb.sem, 1)
                        dve.wait_ge(ga_sb.sem, ga_sb.at(f))
                        dve.wait_ge(hT_ps.sem, hT_ps.at(back(f, 1)))
                        nc.vector.scalar_tensor_tensor(gb[0:C, :], ga[0:C, :], 0.5, ps[0:C, 7, 0:HID],
                                                                  ALU.mult, ALU.mult).then_inc(gb_sb.sem, 1)
                        c = [0]

                        def chosen(ins):
                            ins.then_inc(pick.sem, 1)
                            c[0] += 1
                            dve.wait_ge(pick.sem, pick.at(f, c[0]))
                        dve.wait_ge(place.sem, place.at(back(f, 1)))
                        chosen(nc.vector.reciprocal(rse[0:C, :], se[0:C, :]))
                        chosen(nc.vector.tensor_scalar(sc[0:C, :], ex[0:C, :], rse[0:C, :], None, ALU.mult))
                        chosen(nc.vector.tensor_tensor(met[0:C, :], sc[0:C, :], bias_t[0:C, :], ALU.add))
                        alone(dve)
                        chosen(nc.vector.max(v8[0:C, :], met[0:C, :]))
                        alone(dve)
                        chosen(nc.vector.max_index(i8[0:C, :], v8[0:C, :], met[0:C, :]))
                        chosen(nc.vector.tensor_copy(i2[0:C, :], i8[0:C, 0:2]))
                        for k in range(2):
                            chosen(nc.vector.tensor_scalar(oh[0:C, k, :], iota8[0:C, :], i2[0:C, k:k + 1], None,
                                                           ALU.is_equal))
                        dve.wait_ge(rank_ps.sem, rank_ps.at(back(f, 1)))
                        nc.vector.tensor_tensor(m16[0:C, :], oh[0:C, 0, :], oh[0:C, 1, :], ALU.add).then_inc(m16_sb.sem, 1)
                        dve.wait_ge(scattered.of(back(f, 2)), scattered.at(back(f, 2)))
                        for k in range(2):
                            chosen(nc.vector.scalar_tensor_tensor(junk[0:C, :], sc[0:C, :], 1.0, oh[0:C, k, :],
                                                                  ALU.mult, ALU.mult,
                                                                  accum_out=entry[k][f[1] % 2][0:C, 1:2]))
                        chosen(nc.vector.tensor_scalar(tokf[:], tokf[:], float(C), None, ALU.add))
                        for k in range(2):
                            last = nc.vector.tensor_copy(entry[k][f[1] % 2][0:C, 0:1].bitcast(I32), tokf[0:C, :])
                        chosen(last)
                        dve.wait_ge(hT_hi.sem, hT_hi.at(f))
                        dve.wait_ge(dn_ps.sem, dn_ps.at(back(f, 1)))
                        lo_part(hT, 4, HW).then_inc(hT_lo.sem, 1)
                        dve.wait_ge(dn_ps.sem, dn_ps.at(f))
                        dve.wait_ge(h3_out.of(back(f, 2)), h3_out.at(back(f, 2)))
                        nc.vector.tensor_tensor(h3[f[1] % 2][0:C, :], ps[0:C, 6, :], h2[f[1] % 2][0:C, :],
                                                           ALU.add).then_inc(h3_sb.sem, 1)
                    if has(1):
                        dve.wait_ge(pv_ps.sem, pv_ps.at(a))
                        dve.wait_ge(aT_ps.sem, aT_ps.at(back(a, 1)))
                        av = ps[0:C, 2:4, 0:G * (HD + 1)].rearrange("p g (j d) -> p g j d", j=G)
                        nc.vector.reciprocal(rden[0:C, :].rearrange("p (g j) -> p g j", g=NKV),
                                                          av[:, :, :, HD]).then_inc(rden_sb.sem, 1)
                        dve.wait_ge(rden_sb.sem, rden_sb.at(a))
                        attn_v = attn[0:C, :, :].rearrange("p (g j) d -> p g j d", g=NKV)
                        rd_v = rden[0:C, :].rearrange("p (g j) -> p g j", g=NKV)
                        for g in range(NKV):
                            last = nc.vector.tensor_tensor(attn_v[:, g], av[:, g, :, 0:HD],
                                                           rd_v[:, g, :, None].to_broadcast([C, G, HD]), ALU.mult)
                        last.then_inc(attn_sb.sem, 1)
                    if has(0):
                        dve.wait_ge(zt_ps.sem, zt_ps.at(t))
                        w = C + 1 - 96
                        nc.vector.reciprocal(
                            rz[:, :], ps[:, 4, 0:KC * w].rearrange("p (k w) -> p k w", k=KC)[:, :, w - 1]).then_inc(rz_sb.sem, 1)
                        dve.wait_ge(rz_sb.sem, rz_sb.at(t))
                        dve.wait_ge(bc_ps.sem, bc_ps.at(back(t, 1)))
                        nc.vector.tensor_tensor(diag[:, :, :], ident[:, None, :].to_broadcast([P, KC, P]),
                                                             rz[:, :, None].to_broadcast([P, KC, P]), ALU.mult).then_inc(diag_sb.sem, 1)
                    if has(1):
                        dve.wait_ge(aT_hi.sem, aT_hi.at(a))
                        dve.wait_ge(wo_ps.sem, wo_ps.at(back(a, 1)))
                        lo_part(aT, 5, P).then_inc(aT_lo.sem, 1)
                    if has(2):
                        c2 = [0]

                        def placed(ins):
                            ins.then_inc(place.sem, 1)
                            c2[0] += 1
                            dve.wait_ge(place.sem, place.at(f, c2[0]))
                        dve.wait_ge(rank_ps.sem, rank_ps.at(f))
                        placed(nc.vector.tensor_tensor(posb[0:C, :], ps[0:C, 1, 0:E], base[0:C, :], ALU.add))
                        placed(nc.vector.tensor_tensor(base[:, :], ps[:, 1, E:2 * E], base[:, :], ALU.add))
                        for k in range(2):
                            placed(nc.vector.scalar_tensor_tensor(junk[0:C, :], posb[0:C, :], 1.0, oh[0:C, k, :],
                                                                  ALU.mult, ALU.mult, accum_out=slotf[0:C, k:k + 1]))
                        placed(nc.vector.tensor_copy(slot[f[1] % 2][0:C, :], slotf[0:C, :]))
                    if has(0):
                        dve.wait_ge(bc_ps.sem, bc_ps.at(t))
                        dve.wait_ge(hz_sb.sem, hz_sb.at(t))
                        dve.wait_ge(h2_sb.sem, h2_sb.at(back(t, 2)))
                        nc.vector.tensor_tensor(h[p][0:C, :], ps[0:C, 7, :], hz[0:C, :], ALU.mult).then_inc(h_sb.sem, 1)
                        dve.wait_ge(h_sb.sem, h_sb.at(t))
                        nc.vector.bn_stats(st1[0:C, :], h[p][0:C, :]).then_inc(st1_sb.sem, 1)
                        dve.wait_ge(st1_sb.sem, st1_sb.at(t))
                        dve.wait_ge(ve1_sb.sem, ve1_sb.at(back(t, 1)))
                        alone(dve)
                        nc.vector.bn_aggr(ag1[0:C, :], st1[0:C, :]).then_inc(ag1_sb.sem, 1)
                        dve.wait_ge(rs1_sb.sem, rs1_sb.at(t))
                        dve.wait_ge(xT_ps.sem, xT_ps.at(back(t, 1)))
                        nc.vector.tensor_scalar(xn[0:C, :], h[p][0:C, :], ag1[0:C, 0:1], rs1[0:C, :],
                                                           ALU.subtract, ALU.mult).then_inc(xn_sb.sem, 1)
                    if has(1):
                        dve.wait_ge(wo_ps.sem, wo_ps.at(a))
                        dve.wait_ge(h_sb.sem, h_sb.at(a))
                        dve.wait_ge(h3_sb.sem, h3_sb.at(back(a, 2)))
                        nc.vector.tensor_tensor(h2[pa][0:C, :], ps[0:C, 6, :], h[pa][0:C, :], ALU.add).then_inc(h2_sb.sem, 1)
                        dve.wait_ge(h2_sb.sem, h2_sb.at(a))
                        nc.vector.bn_stats(st2[0:C, :], h2[pa][0:C, :]).then_inc(st2_sb.sem, 1)
                        dve.wait_ge(st2_sb.sem, st2_sb.at(a))
                        dve.wait_ge(ve2_sb.sem, ve2_sb.at(back(a, 1)))
                        alone(dve)
                        nc.vector.bn_aggr(ag2[0:C, :], st2[0:C, :]).then_inc(ag2_sb.sem, 1)
                        dve.wait_ge(rs2_sb.sem, rs2_sb.at(a))
                        dve.wait_ge(y_out.of(back(a, 2)), y_out.at(back(a, 2)))
                        nc.vector.tensor_scalar(y[pa][0:C, :], h2[pa][0:C, :], ag2[0:C, 0:1], rs2[0:C, :],
                                                          ALU.subtract, ALU.mult).then_inc(y_sb.sem, 1)
                each_step(dve, step)

            @block.gpsimd
            def _(pool):
                last_entry = pool.to_reg(REGIONS - 1)

                def step(t, has, n):
                    def cast(b):
                        pool.wait_ge(x_in.of(b), x_in.at(b))
                        pool.wait_ge(mx_ps.sem, mx_ps.at(back(b, 2)))
                        alone(pool)
                        nc.gpsimd.tensor_copy(qk_r[b[1] % 2][0:C, :, :], X[b[1] % 2][0:C, 0:2, :]).then_inc(qkr_r.sem, 1)
                    if n == 0:
                        cast(t)
                    if has(3):
                        g = back(t, 3)
                        pool.wait_ge(pick.sem, pick.at(g))
                        pool.wait_ge(place.sem, place.at(g))
                        for k in range(2):
                            alone(pool)
                            nc.gpsimd.indirect_dma_start(
                                routed, bass.IndirectOffsetOnAxis(ap=slot[g[1] % 2][0:C, k:k + 1], axis=0),
                                entry[k][g[1] % 2][0:C, :], None, bounds_check=last_entry, oob_is_err=False).then_inc(scattered.of(g), 16)
                    if has(-1):
                        cast(back(t, -1))
                    if has(1):
                        pool.wait_ge(rope_sb.sem, rope_sb.at(back(t, 1)))
                        pool.wait_ge(rT_ps.sem, rT_ps.at(back(t, 2)))
                        alone(pool)
                        nc.gpsimd.tensor_tensor(out=qkr[0:C, :], in0=rc[0:C, :], in1=rsn[0:C, :],
                                                              op=ALU.add).then_inc(rope_add.sem, 1)

                    def rstd(b, aggr, ve, rs, aggr_sb, ve_done, rs_done, rs_used):
                        pool.wait_ge(aggr_sb.sem, aggr_sb.at(b))
                        pool.wait_ge(rs_used.sem, rs_used.at(back(b, 1)))
                        alone(pool)
                        nc.gpsimd.tensor_scalar(ve[0:C, :], aggr[0:C, 1:2], EPS, None, ALU.add).then_inc(ve_done.sem, 1)
                        pool.wait_ge(ve_done.sem, ve_done.at(b))
                        alone(pool)
                        nc.gpsimd.tensor_tensor(out=rs[0:C, :], in0=ve[0:C, :], in1=mhalf[0:C, :],
                                                             op=ALU.pow).then_inc(rs_done.sem, 1)
                    if has(0):
                        rstd(t, ag1, ve1, rs1, ag1_sb, ve1_sb, rs1_sb, xn_sb)
                    if has(1):
                        rstd(back(t, 1), ag2, ve2, rs2, ag2_sb, ve2_sb, rs2_sb, y_sb)
                each_step(pool, step)
                pool.wait_ge(scattered.of((0, NB - 1)), scattered.at((0, NB - 1)))
                pool.wait_ge(scattered.of((0, NB - 2)), scattered.at((0, NB - 2)))

        tower.close()

        group_row = sbuf("group_row", [1, NG], I32)
        group_expert = sbuf("group_expert", [1, NG], I32)
        with ExitStack() as c1:
            groups = sbuf("groups", [1, E], F32, c1)
            groups_i = sbuf("groups_i", [1, E], I32, c1)
            upto = sbuf("upto", [1, E], F32, c1)
            skip = sbuf("skip", [1, E], F32, c1)
            number = sbuf("number", [1, NG], F32, c1)
            expert_f = sbuf("expert_f", [1, NG], F32, c1)
            row_f = sbuf("row_f", [1, NG], F32, c1)
            passed = sbuf("passed", [1, NG], F32, c1)
            p_iota, p_dve = (c1.enter_context(nc.semaphore(n)) for n in ("p_iota", "p_dve"))
            with nc.Block() as block:
                @block.gpsimd
                def _(pool):
                    nc.gpsimd.iota(number[:], [[1, NG]], base=0, channel_multiplier=0,
                                   allow_small_or_imprecise_dtypes=True).then_inc(p_iota, 1)
                    nc.gpsimd.iota(skip[:], [[CAP, E]], base=0, channel_multiplier=0,
                                   allow_small_or_imprecise_dtypes=True).then_inc(p_iota, 1)

                @block.vector
                def _(dve):
                    done = [0]

                    def then(ins):
                        ins.then_inc(p_dve, 1)
                        done[0] += 1
                        dve.wait_ge(p_dve, done[0])
                    dve.wait_ge(p_iota, 2)
                    then(nc.vector.tensor_tensor(groups[:], base[0:1, :], skip[:], ALU.subtract))
                    then(nc.vector.tensor_scalar(groups[:], groups[:], float(GROUP - 1), None, ALU.add))
                    then(nc.vector.tensor_copy(groups_i[:], groups[:]))
                    then(nc.vector.tensor_scalar(groups_i[:], groups_i[:], GROUP.bit_length() - 1, None,
                                                 ALU.logical_shift_right))
                    then(nc.vector.tensor_copy(groups[:], groups_i[:]))
                    then(nc.vector.tensor_copy(upto[:, 0:1], groups[:, 0:1]))
                    for i in range(1, E):
                        then(nc.vector.tensor_tensor(upto[:, i:i + 1], upto[:, i - 1:i], groups[:, i:i + 1], ALU.add))
                    then(nc.vector.tensor_scalar(skip[:], groups[:], -float(GROUP), float(CAP), ALU.mult, ALU.add))
                    then(nc.vector.tensor_scalar(row_f[:], number[:], float(GROUP), None, ALU.mult))
                    then(nc.vector.memset(expert_f[:], 0.0))
                    for i in range(E):
                        then(nc.vector.tensor_scalar(passed[:], number[:], upto[:, i:i + 1], None, ALU.is_ge))
                        then(nc.vector.tensor_tensor(expert_f[:], expert_f[:], passed[:], ALU.add))
                        then(nc.vector.scalar_tensor_tensor(row_f[:], passed[:], skip[:, i:i + 1], row_f[:],
                                                            ALU.mult, ALU.add))
                    then(nc.vector.tensor_scalar(expert_f[:], expert_f[:], float(E - 1), None, ALU.min))
                    then(nc.vector.tensor_scalar(row_f[:], row_f[:], float(E * CAP), None, ALU.min))
                    then(nc.vector.tensor_copy(group_expert[:], expert_f[:]))
                    then(nc.vector.tensor_copy(group_row[:], row_f[:]))

        with ExitStack() as c2:
            def pair(name, shape, dt=F32):
                return [sbuf(f"{name}{p}", shape, dt, c2) for p in range(2)]

            raw1 = sbuf("raw1", [P, KC, HID], F32, c2)
            raw3 = sbuf("raw3", [P, KC, HID], F32, c2)
            raw2 = sbuf("raw2", [HW, HC, D], F32, c2)
            raws = (raw1, raw3, raw2)
            W = [tuple((sbuf(f"e{n}_hi{p}", r.shape, F32R, c2), sbuf(f"e{n}_lo{p}", r.shape, F32R, c2))
                       for n, r in enumerate(raws)) for p in range(2)]
            entries = pair("entries", [P, GROUP_TILES, ENTRY])
            rows, scaled = pair("rows", [P, D]), pair("scaled", [P, D])
            rT = pair("rT_hi", [P, KC, P], F32R), pair("rT_lo", [P, KC, P], F32R)
            th, ga = sbuf("eth", [P, HID], F32, c2), sbuf("ega", [P, HID], F32, c2)
            gb = pair("egb", [P, HID])
            uT = (sbuf("uT_hi", [HW, HC, P], F32R, c2), sbuf("uT_lo", [HW, HC, P], F32R, c2))
            res = pair("res", [P, D])

            def tiles(name, per=1):
                return Signal(c2.enter_context(nc.semaphore(name)), per)

            def pair_of(name):
                return DmaSignal(*(c2.enter_context(nc.semaphore(f"{name}_{p}")) for p in range(2)))

            entries_in, rows_in = pair_of("entries_in"), pair_of("rows_in")
            w_in = [pair_of(f"w_in{n}") for n in range(3)]
            added = tiles("added", 16)
            rT_ps, u_ps, uT_ps, d_ps = tiles("t_rT_ps"), tiles("t_u_ps", 2), tiles("t_uT_ps"), tiles("t_d_ps")
            scaled_sb, rT_hi, th_sb, uT_hi = (tiles("t_" + n) for n in ("scaled_sb", "rT_hi", "th_sb", "uT_hi"))
            rT_lo, ga_sb, gb_sb, uT_lo, res_sb = (tiles("t_" + n) for n in ("rT_lo", "ga_sb", "gb_sb", "uT_lo", "res_sb"))
            w_hi, w_lo = [tiles(f"w_hi{n}") for n in range(3)], [tiles(f"w_lo{n}") for n in range(3)]
            cleared = c2.enter_context(nc.semaphore("cleared"))

            T = GROUP_TILES

            def tile_of(group, i):
                j, off = group
                return (T * j, T * off + i)

            def each_group(eng, work):
                work((0, 0), True, False)
                work((0, 1), False, False)
                with eng.Fori(1, NG // 2 - 1) as j:
                    work((j, 0), False, False)
                    work((j, 1), False, False)
                work((0, NG - 2), False, False)
                work((0, NG - 1), False, True)

            with nc.Block() as block:
                @block.sync
                def _(sp):
                    def at(table, group):
                        n = 2 * group[0] + group[1]
                        return table[0:1, n:n + 1] if isinstance(n, int) else table[0:1, bass.ds(n, 1)]

                    def fetch(group):
                        sp.wait_ge(added.sem, added.at(tile_of(back(group, 2), T - 1)))
                        alone(sp)
                        row = sp.value_load(at(group_row, group), min_val=0, max_val=E * CAP)
                        sp.dma_start(entries[group[1] % 2][:], routed[bass.ds(row, GROUP), :].rearrange(
                            "(p i) c -> p i c", p=P)).then_inc(entries_in.of(group), 16)
                        ex = sp.value_load(at(group_expert, group), min_val=0, max_val=E - 1)
                        for n, (src, pp) in enumerate(((w1, P), (w3, P), (w2, HW))):
                            sp.wait_ge(w_lo[n].sem, w_lo[n].at(back(group, 1)))
                            alone(sp)
                            sp.dma_start(raws[n][:], src[bass.ds(ex, 1)].rearrange(
                                "o (k p) h -> p (o k) h", p=pp)).then_inc(w_in[n].of(group), 16)

                    def work(group, first, last):
                        if first:
                            fetch(group)
                        if not last:
                            fetch(back(group, -1))
                    each_group(sp, work)

                @block.tensor
                def _(pe):
                    def cut(dst, lhs, rhs, width, rows_):
                        for k in range(KC):
                            for i, (a, b) in enumerate(((0, 0), (1, 0), (0, 1))):
                                ins = nc.tensor.matmul(dst, lhs[a][:rows_, k, :], rhs[b][:rows_, k, 0:width],
                                                       start=(k == 0 and i == 0), stop=(k == KC - 1 and i == 2))
                        return ins

                    def turn_rows(group, i):
                        t = tile_of(group, i)
                        pe.wait_ge(scaled_sb.sem, scaled_sb.at(t))
                        pe.wait_ge(rT_lo.sem, rT_lo.at(back(t, 2)))
                        for k in range(KC):
                            last = nc.tensor.transpose(ps[:, i % 2, k * P:(k + 1) * P],
                                                       scaled[i % 2][:, k * P:(k + 1) * P], ident[:])
                        last.then_inc(rT_ps.sem, 1)

                    def down(group, i):
                        q, t = group[1] % 2, tile_of(group, i)
                        pe.wait_ge(gb_sb.sem, gb_sb.at(t))
                        pe.wait_ge(uT_lo.sem, uT_lo.at(back(t, 1)))
                        for k in range(HC):
                            last = nc.tensor.transpose(ps[0:HW, 6, k * P:(k + 1) * P],
                                                       gb[i % 2][:, k * HW:(k + 1) * HW], ident[:])
                        last.then_inc(uT_ps.sem, 1)
                        pe.wait_ge(uT_lo.sem, uT_lo.at(t))
                        if i == 0:
                            pe.wait_ge(w_lo[2].sem, w_lo[2].at(group))
                        pe.wait_ge(res_sb.sem, res_sb.at(back(t, 1)))
                        cut(ps[:, 7, :], uT, W[q][2], D, HW).then_inc(d_ps.sem, 1)

                    def work(group, first, last):
                        q = group[1] % 2
                        if first:
                            turn_rows(group, 0)
                        for i in range(T):
                            t = tile_of(group, i)
                            if i == T - 1 and not last:
                                turn_rows(back(group, -1), 0)
                            elif i < T - 1:
                                turn_rows(group, i + 1)
                            if i == 0:
                                pe.wait_ge(w_lo[0].sem, w_lo[0].at(group))
                                pe.wait_ge(w_lo[1].sem, w_lo[1].at(group))
                            pe.wait_ge(rT_lo.sem, rT_lo.at(t))
                            b = 2 + 2 * (i % 2)
                            pe.wait_ge(ga_sb.sem, ga_sb.at(back(t, 2)))
                            lhs = (rT[0][i % 2], rT[1][i % 2])
                            cut(ps[:, b, 0:HID], lhs, W[q][0], HID, P).then_inc(u_ps.sem, 1)
                            pe.wait_ge(gb_sb.sem, gb_sb.at(back(t, 2)))
                            cut(ps[:, b + 1, 0:HID], lhs, W[q][1], HID, P).then_inc(u_ps.sem, 1)
                            if i > 0:
                                down(group, i - 1)
                            elif not first:
                                down(back(group, 1), T - 1)
                        if last:
                            down(group, T - 1)
                    each_group(pe, work)

                @block.scalar
                def _(act):
                    def cut_weight(group, n):
                        act.wait_ge(w_in[n].of(group), w_in[n].at(group))
                        act.wait_ge(d_ps.sem, d_ps.at(tile_of(back(group, 2), T - 1)))
                        nc.scalar.activation(W[group[1] % 2][n][0][:], raws[n][:], ACT.Copy).then_inc(w_hi[n].sem, 1)

                    def scale_rows(group, i):
                        t = tile_of(group, i)
                        act.wait_ge(rows_in.of(t), rows_in.at(t))
                        act.wait_ge(rT_ps.sem, rT_ps.at(back(t, 2)))
                        nc.scalar.activation(scaled[i % 2][:], rows[i % 2][:], ACT.Copy,
                                                            scale=entries[group[1] % 2][:, i, 1:2]).then_inc(scaled_sb.sem, 1)

                    def rows_hi(t, i):
                        act.wait_ge(rT_ps.sem, rT_ps.at(t))
                        act.wait_ge(u_ps.sem, u_ps.at(back(t, 2)))
                        nc.scalar.activation(rT[0][i % 2][:], ps[:, i % 2, :].rearrange(
                            "p (k c) -> p k c", k=KC), ACT.Copy).then_inc(rT_hi.sem, 1)

                    def hidden_hi(t):
                        act.wait_ge(uT_ps.sem, uT_ps.at(t))
                        act.wait_ge(d_ps.sem, d_ps.at(back(t, 1)))
                        nc.scalar.activation(uT[0][:], ps[0:HW, 6, :].rearrange(
                            "p (k c) -> p k c", k=HC), ACT.Copy).then_inc(uT_hi.sem, 1)

                    def work(group, first, last):
                        if first:
                            scale_rows(group, 0)
                            scale_rows(group, 1)
                            for n in range(3):
                                cut_weight(group, n)
                            rows_hi(tile_of(group, 0), 0)
                        for i in range(T):
                            t = tile_of(group, i)
                            if not (last and i == T - 1):
                                rows_hi(back(t, -1), i + 1)
                            act.wait_ge(u_ps.sem, u_ps.at(t, 1))
                            act.wait_ge(ga_sb.sem, ga_sb.at(back(t, 1)))
                            nc.scalar.activation(th[:], ps[:, 2 + 2 * (i % 2), 0:HID], ACT.Tanh, scale=0.5).then_inc(th_sb.sem, 1)
                            if not (first and i == 0):
                                hidden_hi(back(t, 1))
                            if i < T - 2:
                                scale_rows(group, i + 2)
                            elif not last:
                                scale_rows(back(group, -1), i + 2 - T)
                            if i > 0 and not last:
                                cut_weight(back(group, -1), i - 1)
                        if last:
                            hidden_hi(tile_of(group, T - 1))
                    each_group(act, work)

                @block.vector
                def _(dve):
                    for p in range(2):
                        nc.vector.memset(rows[p][:], 0.0).then_inc(cleared, 1)

                    def cut_weight(group, n):
                        dve.wait_ge(w_hi[n].sem, w_hi[n].at(group))
                        nc.vector.tensor_tensor(W[group[1] % 2][n][1][:], raws[n][:],
                                                             W[group[1] % 2][n][0][:].bitcast(F32), ALU.subtract).then_inc(w_lo[n].sem, 1)

                    def rows_lo(t, i):
                        dve.wait_ge(rT_hi.sem, rT_hi.at(t))
                        dve.wait_ge(u_ps.sem, u_ps.at(back(t, 2)))
                        nc.vector.tensor_tensor(rT[1][i % 2][:], ps[:, i % 2, :].rearrange(
                            "p (k c) -> p k c", k=KC), rT[0][i % 2][:].bitcast(F32), ALU.subtract).then_inc(rT_lo.sem, 1)

                    def finish(t, i):
                        dve.wait_ge(uT_hi.sem, uT_hi.at(t))
                        dve.wait_ge(d_ps.sem, d_ps.at(back(t, 1)))
                        nc.vector.tensor_tensor(uT[1][:], ps[0:HW, 6, :].rearrange(
                            "p (k c) -> p k c", k=HC), uT[0][:].bitcast(F32), ALU.subtract).then_inc(uT_lo.sem, 1)
                        dve.wait_ge(d_ps.sem, d_ps.at(t))
                        dve.wait_ge(added.sem, added.at(back(t, 2)))
                        nc.vector.tensor_copy(res[i % 2][:], ps[:, 7, :]).then_inc(res_sb.sem, 1)

                    def work(group, first, last):
                        if first:
                            cut_weight(group, 2)
                            rows_lo(tile_of(group, 0), 0)
                        for i in range(T):
                            t = tile_of(group, i)
                            if not (last and i == T - 1):
                                rows_lo(back(t, -1), i + 1)
                            dve.wait_ge(th_sb.sem, th_sb.at(t))
                            dve.wait_ge(gb_sb.sem, gb_sb.at(back(t, 1)))
                            b = 2 + 2 * (i % 2)
                            nc.vector.scalar_tensor_tensor(ga[:], th[:], 1.0, ps[:, b, 0:HID],
                                                                      ALU.add, ALU.mult).then_inc(ga_sb.sem, 1)
                            dve.wait_ge(ga_sb.sem, ga_sb.at(t))
                            dve.wait_ge(u_ps.sem, u_ps.at(t))
                            dve.wait_ge(uT_ps.sem, uT_ps.at(back(t, 2)))
                            nc.vector.scalar_tensor_tensor(gb[i % 2][:], ga[:], 0.5, ps[:, b + 1, 0:HID],
                                                                      ALU.mult, ALU.mult).then_inc(gb_sb.sem, 1)
                            if not (first and i == 0):
                                finish(back(t, 1), i + 1)
                            if i == T - 1 and not last:
                                cut_weight(back(group, -1), 2)
                        if last:
                            finish(tile_of(group, T - 1), T - 1)
                    each_group(dve, work)

                @block.gpsimd
                def _(pool):
                    last_token = pool.to_reg(TOKENS - 1)

                    def cut_weight(group, n):
                        pool.wait_ge(w_hi[n].sem, w_hi[n].at(group))
                        alone(pool)
                        nc.gpsimd.tensor_tensor(out=W[group[1] % 2][n][1][:], in0=raws[n][:],
                                                             in1=W[group[1] % 2][n][0][:].bitcast(F32),
                                                             op=ALU.subtract).then_inc(w_lo[n].sem, 1)

                    def gather(group, i):
                        t = tile_of(group, i)
                        pool.wait_ge(entries_in.of(group), entries_in.at(group))
                        pool.wait_ge(scaled_sb.sem, scaled_sb.at(back(t, 2)))
                        alone(pool)
                        nc.gpsimd.indirect_dma_start(
                            rows[i % 2][:], None, normed, bass.IndirectOffsetOnAxis(
                                ap=entries[group[1] % 2][:, i, 0:1].bitcast(I32), axis=0),
                            bounds_check=last_token, oob_is_err=False).then_inc(rows_in.of(t), 16)

                    def add_rows(group, i):
                        t = tile_of(group, i)
                        pool.wait_ge(res_sb.sem, res_sb.at(t))
                        pool.wait_ge(added.sem, added.at(back(t, 1)))
                        alone(pool)
                        nc.gpsimd.indirect_dma_start(
                            out, bass.IndirectOffsetOnAxis(ap=entries[group[1] % 2][:, i, 0:1].bitcast(I32), axis=0),
                            res[i % 2][:], None, bounds_check=last_token, oob_is_err=False,
                            compute_op=ALU.add).then_inc(added.sem, 16)

                    pool.wait_ge(cleared, 2)

                    def work(group, first, last):
                        if first:
                            gather(group, 0)
                            gather(group, 1)
                            cut_weight(group, 0)
                            cut_weight(group, 1)
                        for i in range(T):
                            if i < T - 2:
                                gather(group, i + 2)
                            elif not last:
                                gather(back(group, -1), i + 2 - T)
                            if i > 0:
                                add_rows(group, i - 1)
                            elif not first:
                                add_rows(back(group, 1), T - 1)
                            if i in (1, 2) and not last:
                                cut_weight(back(group, -1), i - 1)
                        if last:
                            add_rows(group, T - 1)
                            pool.wait_ge(added.sem, added.at(tile_of(group, T - 1)))
                    each_group(pool, work)


_INS = ["x", "L0_attn_Wq", "L0_attn_Wk", "L0_attn_Wv", "L0_attn_Wo", "L0_ffn_gate_w", "L0_ffn_w1", "L0_ffn_w2",
        "L0_ffn_w3", "L0_ffn_sw1", "L0_ffn_sw2", "L0_ffn_sw3", "L0_ffn_expert_bias"]


def rope_tables(tokens, width):
    import numpy as np

    inv_freq = (1.0 / np.float32(10000.0) ** (np.arange(0, width, 2, dtype=np.float32) / np.float32(width))).astype(np.float32)
    freqs = (np.arange(tokens, dtype=np.float32)[:, None] * inv_freq[None, :]).astype(np.float32)
    cos, sin = np.cos(freqs).astype(np.float32), np.sin(freqs).astype(np.float32)
    return np.concatenate([cos, cos], 1), np.concatenate([-sin, sin], 1)


def kernel(**inputs):
    import numpy as np
    import concourse.bacc as bacc
    from concourse import mybir as _mybir
    from concourse.bass_utils import run_bass_kernel_spmd

    nc = bacc.Bacc("TRN2", target_bir_lowering=False, num_devices=1)
    arrays, args = {}, []
    for name in _INS:
        arrays[f"in_{name}"] = np.ascontiguousarray(inputs[name])
    nb, c3, d = inputs["x"].shape
    arrays["rope_cos"], arrays["rope_sin"] = rope_tables(c3 // 3, 64)
    for name, a in arrays.items():
        args.append(nc.dram_tensor(name, a.shape, _mybir.dt.from_np(a.dtype), kind="ExternalInput").ap())
    out = nc.dram_tensor("out_dram", (nb * (c3 // 3), d), _mybir.dt.float32, kind="ExternalOutput").ap()
    audio_tower(nc, *args, out)
    r = run_bass_kernel_spmd(nc, [arrays], core_ids=[0])
    return r.results[0]["out_dram"].reshape(nb, c3 // 3, d)
```

```python
from contextlib import ExitStack

import concourse.bass as bass
from concourse import mybir

F32 = mybir.dt.float32
F32R = mybir.dt.float32r
BF16 = mybir.dt.bfloat16
I32 = mybir.dt.int32
U32 = mybir.dt.uint32
ALU = mybir.AluOpType
ACT = mybir.ActivationFunctionType
AX = mybir.AxisListType

P = 128
PASSES = ((0, 0), (0, 1), (1, 0))
EPS = 1e-5
GROUP_TILES = 4
GROUP = GROUP_TILES * P


class Signal:

    def __init__(self, sem, per=1, batches=None):
        self.sem, self.per, self.batches = sem, per, batches

    def at(self, batch, k=None):
        j, off = batch
        if self.batches and isinstance(j, int) and 2 * j + off >= self.batches:
            j, off, k = 0, self.batches - 1, None
        value = 2 * self.per * j + (self.per * off + (self.per if k is None else k))
        return max(value, 0) if isinstance(value, int) else value


class DmaSignal:

    def __init__(self, even, odd, per=1):
        self.sems, self.per = (even, odd), per

    def of(self, batch):
        return self.sems[batch[1] % 2]

    def at(self, batch):
        value = 16 * self.per * batch[0] + 16 * self.per * (batch[1] // 2 + 1)
        return max(value, 0) if isinstance(value, int) else value


def back(batch, k):
    return (batch[0], batch[1] - k)


def audio_tower(nc, x, wq, wk, wv, wo, gate_w, w1, w2, w3, sw1, sw2, sw3, expert_bias, cos, sin, out):
    NB, C3, D = x.shape
    C = C3 // 3
    E, _, HID = w1.shape
    HD = 64
    NH = wq.shape[0] // HD
    NKV = wk.shape[0] // HD
    G = NH // NKV
    QKV = (NH + 2 * NKV) * HD
    QK = (NH + NKV) * HD
    KC = D // P
    HC = 4
    HW = HID // HC
    HG = HID + E
    TOKENS = NB * C
    CAP = -(-TOKENS // GROUP) * GROUP + GROUP
    ENTRY = 2
    NOWHERE = 1 << 22
    NG = (2 * TOKENS - E) // GROUP + E
    NG += NG % 2
    STEPS_IN, STEPS_OUT = 6, 5
    LAG = 3
    VW = HD + 1
    assert NB % 2 == 0 and D == 512 and HW * HC == HID and NH == 8 and NKV == 2

    REGIONS = -(-(E * CAP + GROUP) // P) * P
    routed = nc.dram_tensor("routed_entries", (REGIONS, ENTRY), F32).ap()
    normed = nc.dram_tensor("normed_rows", (TOKENS, D), F32).ap()

    with ExitStack() as ctx:
        def sem(name):
            return ctx.enter_context(nc.semaphore(name))

        def sbuf(name, shape, dt=F32, where=ctx):
            return where.enter_context(nc.sbuf_tensor(name, shape, dt))

        def signal(name, per=1):
            return Signal(sem(name), per, NB)

        def dma_signal(name, per=1):
            return DmaSignal(sem(name + "_even"), sem(name + "_odd"), per)

        ps = ctx.enter_context(nc.psum_tensor("ps", [P, 8, 512], F32))
        ident = sbuf("ident", [P, P])
        base = sbuf("base", [P, E])

        tower = ctx.enter_context(ExitStack())

        def resident(name, shape):
            return (sbuf(name + "_hi", shape, F32R, tower), sbuf(name + "_lo", shape, F32R, tower))

        wqkv = resident("wqkv", [P, KC, QKV])
        woT = resident("woT", [P, KC, D])
        w1g = resident("w1g", [P, KC, HG])
        w3s = resident("w3s", [P, KC, HID])
        w2s = resident("w2s", [HW, HC, D])
        cos_t = sbuf("cos_t", [P, HD], F32, tower)
        sin_t = sbuf("sin_t", [P, HD], F32, tower)
        bias_t = sbuf("bias_t", [P, E], F32, tower)
        iota8 = sbuf("iota8", [P, E], F32, tower)
        tri = sbuf("tri", [P, P], BF16, tower)
        ones16 = sbuf("ones16", [P, P], BF16, tower)
        mhalf = sbuf("mhalf", [P, 1], F32, tower)
        tokf = sbuf("tokf", [P, 1], F32, tower)
        X = [sbuf(f"X{p}", [P, 3, D], F32, tower) for p in range(2)]
        qk_high = [sbuf(f"qk_high{p}", [P, 2, D], F32R, tower) for p in range(2)]
        qk_low = sbuf("qk_low", [P, 2, D], F32R, tower)
        vaug = [sbuf(f"vaug{p}", [P, NKV, VW], F32, tower) for p in range(2)]
        one_row = sbuf("one_row", [P, KC, P], F32, tower)
        rzT = sbuf("rzT", [P, P], F32, tower)
        vT = [sbuf(f"vT_{part}", [P, KC, C + 1], F32R, tower) for part in ("high", "low")]

        with ExitStack() as c0:
            s_raw, s_const, s_const2, s_pe, s_hi, s_lo, s_set, s_empty = (
                c0.enter_context(nc.semaphore(n)) for n in
                ("s_raw", "s_const", "s_const2", "s_pe", "s_hi", "s_lo", "s_set", "s_empty"))
            raw_q = sbuf("raw_q", [P, KC, D], F32, c0)
            raw_k = sbuf("raw_k", [P, D], F32, c0)
            raw_v = sbuf("raw_v", [P, D], F32, c0)
            raw_o = sbuf("raw_o", [P, KC, D], F32, c0)
            raw_1 = sbuf("raw_1", [P, KC, HG], F32, c0)
            raw_3 = sbuf("raw_3", [P, KC, HID], F32, c0)
            raw_2 = sbuf("raw_2", [HW, HC, D], F32, c0)
            trif = sbuf("trif", [P, P], F32, c0)
            empty = sbuf("empty", [P, REGIONS // P, ENTRY], F32, c0)
            n_loads = [0]
            N_LOADS = NH + 11
            jobs = [(raw_q[:, j, :], wqkv, P * j) for j in range(KC)]
            jobs += [(raw_k[:, :], wqkv, NH * HD), (raw_v[:, :], wqkv, QK)]
            jobs += [(raw_o[:, j, :], woT, P * j) for j in range(KC)]
            direct = [(raw_1, w1g), (raw_3, w3s), (raw_2, w2s)]

            with nc.Block() as block:
                @block.sync
                def _(sp):
                    def load(dst, src):
                        sp.dma_start(dst, src).then_inc(s_raw, 16)
                        n_loads[0] += 1
                    for j in range(G):
                        for g in range(NKV):
                            load(raw_q[g * HD:(g + 1) * HD, j, :], wq[(g * G + j) * HD:(g * G + j + 1) * HD, :])
                    load(raw_k[:, :], wk)
                    load(raw_v[:, :], wv)
                    load(raw_o[:, :, :], wo.rearrange("(j p) d -> p j d", p=P))
                    load(raw_1[:, :, 0:HID], sw1.rearrange("(k p) h -> p k h", p=P))
                    load(raw_1[:, :, HID:HG], gate_w.rearrange("(k p) h -> p k h", p=P))
                    load(raw_3[:, :, :], sw3.rearrange("(k p) h -> p k h", p=P))
                    load(raw_2[:, :, :], sw2.rearrange("(k p) h -> p k h", p=HW))
                    load(cos_t[0:C, :], cos)
                    load(sin_t[0:C, :], sin)
                    sp.wait_ge(s_empty, 2)
                    load(routed.rearrange("(p n) c -> p n c", p=P), empty[:, :, :])
                    load(bias_t[:, :], expert_bias.rearrange("(o e) -> o e", o=1).to_broadcast([P, E]))
                    assert n_loads[0] == N_LOADS
                    sp.wait_ge(s_raw, 16 * N_LOADS)

                @block.gpsimd
                def _(pool):
                    nc.gpsimd.memset(ident[:], 0.0).then_inc(s_const, 1)
                    nc.gpsimd.memset(trif[:], 1.0).then_inc(s_const, 1)
                    nc.gpsimd.iota(iota8[:], [[1, E]], base=0, channel_multiplier=0,
                                   allow_small_or_imprecise_dtypes=True).then_inc(s_const, 1)
                    nc.gpsimd.iota(base[:], [[CAP, E]], base=0, channel_multiplier=0,
                                   allow_small_or_imprecise_dtypes=True).then_inc(s_const, 1)
                    nc.gpsimd.iota(tokf[:], [[1, 1]], base=-C, channel_multiplier=1,
                                   allow_small_or_imprecise_dtypes=True).then_inc(s_const, 1)
                    pool.wait_ge(s_const, 5)
                    nc.gpsimd.affine_select(out=ident[:], in_=ident[:], compare_op=ALU.not_equal, fill=1.0,
                                            base=0, pattern=[[-1, P]], channel_multiplier=1).then_inc(s_const2, 1)
                    nc.gpsimd.affine_select(out=trif[:], in_=trif[:], compare_op=ALU.is_gt, fill=0.0,
                                            base=0, pattern=[[1, P]], channel_multiplier=-1).then_inc(s_const2, 1)

                @block.vector
                def _(dve):
                    nc.vector.memset(empty[:, :, 0].bitcast(I32), NOWHERE).then_inc(s_empty, 1)
                    nc.vector.memset(empty[:, :, 1], 0.0).then_inc(s_empty, 1)
                    nc.vector.memset(ones16[:], 1.0).then_inc(s_set, 1)
                    nc.vector.memset(mhalf[:], -0.5).then_inc(s_set, 1)
                    for p in range(2):
                        nc.vector.memset(qk_high[p][96:P, 1, :].bitcast(F32), 1.0).then_inc(s_set, 1)
                        nc.vector.memset(vaug[p][:, :, HD:VW], 1.0).then_inc(s_set, 1)
                        nc.vector.memset(vT[p][:, :, C:C + 1].bitcast(F32), float(1 - p)).then_inc(s_set, 1)
                    dve.wait_ge(s_const2, 2)
                    nc.vector.tensor_copy(tri[:], trif[:]).then_inc(s_set, 1)
                    for i in range(KC):
                        nc.vector.tensor_copy(one_row[:, i, :],
                                              ident[:, i:i + 1].to_broadcast([P, P])).then_inc(s_set, 1)
                    nc.vector.memset(rzT[:], 0.0).then_inc(s_set, 1)
                    for n, (_, w, col) in enumerate(jobs):
                        dve.wait_ge(s_hi, n + 1)
                        nc.vector.tensor_tensor(w[1][:, :, col:col + P],
                                                ps[:, n % 2, :].rearrange("p (k m) -> p k m", k=KC),
                                                w[0][:, :, col:col + P].bitcast(F32), ALU.subtract).then_inc(s_lo, 1)
                    for n, (raw, w) in enumerate(direct):
                        dve.wait_ge(s_hi, len(jobs) + n + 1)
                        nc.vector.tensor_tensor(w[1][:], raw[:], w[0][:].bitcast(F32), ALU.subtract).then_inc(s_lo, 1)

                @block.tensor
                def _(pe):
                    pe.wait_ge(s_raw, 16 * N_LOADS)
                    pe.wait_ge(s_const2, 2)
                    for n, (src, _, _) in enumerate(jobs):
                        if n >= 2:
                            pe.wait_ge(s_lo, n - 1)
                        for k in range(KC):
                            last = nc.tensor.transpose(ps[:, n % 2, k * P:(k + 1) * P], src[:, k * P:(k + 1) * P],
                                                       ident[:])
                        last.then_inc(s_pe, 1)

                @block.scalar
                def _(act):
                    for n, (_, w, col) in enumerate(jobs):
                        act.wait_ge(s_pe, n + 1)
                        nc.scalar.activation(w[0][:, :, col:col + P],
                                             ps[:, n % 2, :].rearrange("p (k m) -> p k m", k=KC),
                                             ACT.Copy).then_inc(s_hi, 1)
                    act.wait_ge(s_raw, 16 * N_LOADS)
                    for raw, w in direct:
                        nc.scalar.activation(w[0][:], raw[:], ACT.Copy).then_inc(s_hi, 1)

        def pair(name, shape, dt=F32):
            return [sbuf(f"{name}{p}", shape, dt, tower) for p in range(2)]

        def one(name, shape, dt=F32):
            return sbuf(name, shape, dt, tower)

        def parts(name, shape):
            return one(name + "_hi", shape, F32R), one(name + "_lo", shape, F32R)

        mrow = pair("mrow", [KC, P], F32R)
        negmax = pair("negmax", [P, KC])
        e = one("e", [P, KC, D])
        e_cut = parts("e_cut", [P, KC, D])
        vT_full = one("vT_full", [P, KC, C])
        hz = one("hz", [P, D])
        rz = one("rz", [P, KC])
        h = pair("h", [P, D])
        st1, ag1 = one("st1", [P, 6]), one("ag1", [P, 2])
        st2, ag2 = one("st2", [P, 6]), one("ag2", [P, 2])
        ve1, rs1 = one("ve1", [P, 1]), one("rs1", [P, 1])
        ve2, rs2 = one("ve2", [P, 1]), one("rs2", [P, 1])
        xn = one("xn", [P, D])
        xT = parts("xT", [P, KC, P])
        rc = one("rc", [P, QK])
        rsn = one("rsn", [P, QK])
        qkr = one("qkr", [P, QK])
        qkT = parts("qkT", [P, NH // 2 + 1, C])
        capped = one("capped", [P, G * C])
        prob = one("prob", [P, NKV, G * C])
        rden = one("rden", [P, NH])
        attn = one("attn", [P, NH, HD])
        aT = parts("aT", [P, KC, P])
        h2 = pair("h2", [P, D])
        y = pair("y", [P, D])
        yT = parts("yT", [P, KC, P])
        th = one("th", [P, HID])
        ga = one("ga", [P, HID])
        gb = one("gb", [P, HID])
        hT = parts("hT", [P, HC, P])
        h3 = pair("h3", [P, D])
        nl, ex, se, rse = one("nl", [P, 1]), one("ex", [P, E]), one("se", [P, 1]), one("rse", [P, 1])
        sc, met, v8, i8 = one("sc", [P, E]), one("met", [P, E]), one("v8", [P, E]), one("i8", [P, E], U32)
        i2 = one("i2", [P, 2])
        oh = one("oh", [P, 2, E])
        m16 = one("m16", [P, E], BF16)
        junk = one("junk", [P, E])
        posb = one("posb", [P, E])
        slotf = one("slotf", [P, 2])
        slot = pair("slot", [P, 2], I32)
        entry = [pair(f"entry{k}_", [P, ENTRY]) for k in range(2)]

        x_in, row_in, h3_out, y_out = (dma_signal(n) for n in ("x_in", "row_in", "h3_out", "y_out"))
        scattered = dma_signal("scattered", 2)
        wo_ps, xT_ps, vT_ps, mx_ps = signal("wo_ps"), signal("xT_ps"), signal("vT_ps"), signal("mx_ps", KC)
        q_ps, yT_ps, kv_ps, mt_ps = signal("q_ps"), signal("yT_ps"), signal("kv_ps"), signal("mt_ps")
        up_ps, qk_ps, rT_ps, hT_ps = signal("up_ps", 2), signal("qk_ps", KC), signal("rT_ps"), signal("hT_ps")
        s_ps, o_ps, pv_ps = signal("s_ps", 2), signal("o_ps"), signal("pv_ps", 2)
        zt_ps, rzT_ps, rzT_sb = signal("zt_ps"), signal("rzT_ps"), signal("rzT_sb")
        rank_ps, dn_ps, aT_ps, bc_ps = signal("rank_ps"), signal("dn_ps"), signal("aT_ps"), signal("bc_ps")
        xT_hi, vT_hi, yT_hi, v_sb, th_sb = (signal(n) for n in ("xT_hi", "vT_hi", "yT_hi", "v_sb", "th_sb"))
        ex_sb, e_sb, qkT_hi, hT_hi = signal("ex_sb"), signal("e_sb", KC), signal("qkT_hi"), signal("hT_hi")
        tanh_sb, p_sb, hz_sb = signal("tanh_sb", 2), signal("p_sb", 2), signal("hz_sb")
        aT_hi, qk_hi, e_hi23, vT_sb = signal("aT_hi"), signal("qk_hi"), signal("e_hi23", 2), signal("vT_sb")
        h_sb, st1_sb, ag1_sb, xn_sb = signal("h_sb"), signal("st1_sb"), signal("ag1_sb"), signal("xn_sb")
        h2_sb, st2_sb, ag2_sb, y_sb = signal("h2_sb"), signal("st2_sb"), signal("ag2_sb"), signal("y_sb")
        xT_lo, max_sb, mrow_sb, yT_lo = signal("xT_lo"), signal("max_sb", KC), signal("mrow_sb"), signal("yT_lo")
        rope_sb, nl_sb, ga_sb, gb_sb = signal("rope_sb", 3), signal("nl_sb"), signal("ga_sb"), signal("gb_sb")
        qkT_lo, hT_lo, pick, m16_sb = signal("qkT_lo"), signal("hT_lo"), signal("pick", 12), signal("m16_sb")
        rden_sb, attn_sb, rz_sb = signal("rden_sb", 2), signal("attn_sb", 2), signal("rz_sb")
        e_hi01, e_lo = signal("e_hi01", 2), signal("e_lo", KC)
        h3_sb, aT_lo, place = signal("h3_sb"), signal("aT_lo"), signal("place", 5)
        qk_lo, rope_add, vT_lo = signal("qk_lo"), signal("rope_add"), signal("vT_lo")
        ve1_sb, rs1_sb, ve2_sb, rs2_sb = signal("ve1_sb"), signal("rs1_sb"), signal("ve2_sb"), signal("rs2_sb")
        past = sem("past")

        def alone(eng):
            eng.sem_inc(past, 1)

        def product(pe, dst, lhs, rhs, rows, c0, c1, lo, at, between=None):
            for i, (a, b) in enumerate(PASSES):
                if i == 2:
                    if between:
                        between()
                    pe.wait_ge(lo, at)
                for k in range(KC):
                    last = nc.tensor.matmul(dst, lhs[a][:rows, k, 0:C], rhs[b][:rows, k, c0:c1],
                                            start=(k == 0 and i == 0), stop=(k == KC - 1 and i == 2))
            return last

        def each_step(eng, step):
            def static(n):
                step((0, n), lambda lag: 0 <= n - lag < NB, n)
            for n in range(STEPS_IN):
                static(n)
            with eng.Fori(STEPS_IN // 2, (NB - 2) // 2) as j:
                for p in range(2):
                    step((j, p), lambda lag: True, None)
            for n in range(NB - 2, NB + LAG):
                static(n)

        SUMS = C + 1 - 96
        QS = 1.0 / float(C) ** 0.5
        RANKS = D - 2 * E
        CAPF = 50.0
        TANH = 1.0 / (16.0 * CAPF)

        with nc.Block() as block:
            @block.sync
            def _(sp):
                def rows_of(table, batch):
                    row0 = C * (2 * batch[0] + batch[1])
                    return table[row0:row0 + C, :] if isinstance(row0, int) else table[bass.ds(row0, C), :]

                def load(b):
                    sp.wait_ge(qk_lo.sem, qk_lo.at(back(b, 2)))
                    sp.wait_ge(vT_ps.sem, vT_ps.at(back(b, 2)))
                    alone(sp)
                    n = 2 * b[0] + b[1]
                    src = x[n] if isinstance(n, int) else x[bass.ds(n, 1)].rearrange("o c d -> (o c) d")
                    sp.dma_start(X[b[1] % 2][0:C, :, :],
                                 src.rearrange("(a c) d -> c a d", a=3)).then_inc(x_in.of(b), 16)

                def step(t, has, n):
                    f = back(t, 2)
                    if n == 0:
                        load(t)
                    if has(-1):
                        load(back(t, -1))
                    if has(3):
                        g = back(t, 3)
                        sp.wait_ge(h3_sb.sem, h3_sb.at(g))
                        alone(sp)
                        sp.dma_start(rows_of(out, g), h3[g[1] % 2][0:C, :]).then_inc(h3_out.of(g), 16)
                    if has(2):
                        sp.wait_ge(y_sb.sem, y_sb.at(f))
                        alone(sp)
                        sp.dma_start(rows_of(normed, f), y[f[1] % 2][0:C, :]).then_inc(y_out.of(f), 16)
                    if has(0):
                        sp.wait_ge(mrow_sb.sem, mrow_sb.at(t))
                        sp.dma_start(
                            qk_high[t[1] % 2][C:C + 1, 0, :].bitcast(F32).rearrange("o (a b) -> o a b", a=KC),
                            mrow[t[1] % 2][:, :].bitcast(F32)).then_inc(row_in.of(t), 16)
                each_step(sp, step)
                for b in ((0, NB - 2), (0, NB - 1)):
                    sp.wait_ge(h3_out.of(b), h3_out.at(b))
                    sp.wait_ge(y_out.of(b), y_out.at(b))

            @block.tensor
            def _(pe):
                def turn(bank, rows, src):
                    for k in range(KC):
                        last = nc.tensor.transpose(ps[0:rows, bank, k * C:(k + 1) * C],
                                                   src[0:C, k * rows:(k + 1) * rows], ident[0:C, 0:C])
                    return last

                def step(t, has, n):
                    a, f, g = back(t, 1), back(t, 2), back(t, 3)
                    p = t[1] % 2

                    def down_part(k, part, c=0, last=False):
                        return nc.tensor.matmul(ps[0:C, 6, :], hT[c][0:HW, k, 0:C], w2s[part][0:HW, k, 0:D],
                                                start=(k == 0 and part == 0 and c == 0), stop=last)
                    if has(0):
                        pe.wait_ge(qk_hi.sem, qk_hi.at(t))
                        pe.wait_ge(hz_sb.sem, hz_sb.at(a))
                        pe.wait_ge(e_sb.sem, e_sb.at(a))
                        for i in range(2):
                            nc.tensor.matmul(ps[:, i, :], qk_high[p][0:C, 0, i * P:(i + 1) * P], qk_high[p][0:C, 1, :],
                                             start=True, stop=True).then_inc(mx_ps.sem, 1)
                    if has(1):
                        pe.wait_ge(rz_sb.sem, rz_sb.at(a))
                        nc.tensor.transpose(ps[0:KC, 4, KC * SUMS:KC * SUMS + P], rz[:, :],
                                            ident[:, :]).then_inc(rzT_ps.sem, 1)
                    if has(3):
                        down_part(2, 0)
                    if has(2):
                        pe.wait_ge(attn_sb.sem, attn_sb.at(f))
                        pe.wait_ge(tanh_sb.sem, tanh_sb.at(f))
                        turn(5, P, attn[:, :, :].rearrange("p a b -> p (a b)")).then_inc(aT_ps.sem, 1)
                    if has(3):
                        down_part(3, 0)
                    if has(1):
                        pe.wait_ge(rzT_sb.sem, rzT_sb.at(a))
                        pe.wait_ge(tanh_sb.sem, tanh_sb.at(f))
                        pe.wait_ge(gb_sb.sem, gb_sb.at(g))
                        for i in range(KC):
                            last = nc.tensor.matmul(ps[0:C, 7, i * P:(i + 1) * P], one_row[:, i, 0:C],
                                                    rzT[:, :], start=True, stop=True)
                        last.then_inc(bc_ps.sem, 1)
                    if has(0):
                        pe.wait_ge(x_in.of(t), x_in.at(t))
                        pe.wait_ge(attn_sb.sem, attn_sb.at(f))
                        for k in range(KC):
                            last = nc.tensor.transpose(ps[:, 2, k * C:(k + 1) * C],
                                                       X[p][0:C, 2, k * P:(k + 1) * P], ident[0:C, 0:C])
                        last.then_inc(vT_ps.sem, 1)
                    if has(0):
                        for i in range(2, KC):
                            pe.wait_ge(max_sb.sem, max_sb.at(t, i - 1))
                            nc.tensor.matmul(ps[:, i - 2, :], qk_high[p][0:C, 0, i * P:(i + 1) * P],
                                             qk_high[p][0:C, 1, :], start=True, stop=True).then_inc(mx_ps.sem, 1)
                    if has(3):
                        down_part(0, 1)
                    if has(2):
                        pe.wait_ge(aT_hi.sem, aT_hi.at(f))
                        if has(1):
                            pe.wait_ge(h_sb.sem, h_sb.at(a))
                        product(pe, ps[0:C, 7, :], aT, woT, P, 0, D, aT_lo.sem, aT_lo.at(f)).then_inc(wo_ps.sem, 1)
                    if has(1):
                        pe.wait_ge(xn_sb.sem, xn_sb.at(a))
                        pe.wait_ge(attn_sb.sem, attn_sb.at(f))
                        turn(3, P, xn).then_inc(xT_ps.sem, 1)
                    if has(3):
                        for k in range(1, HC):
                            down_part(k, 1)
                        pe.wait_ge(hT_lo.sem, hT_lo.at(g))
                        for k in range(HC):
                            last = down_part(k, 0, c=1, last=(k == HC - 1))
                        last.then_inc(dn_ps.sem, 1)
                    if has(1):
                        pe.wait_ge(xT_hi.sem, xT_hi.at(a))
                        pe.wait_ge(place.sem, place.at(g))
                        product(pe, ps[0:C, 4, :], xT, wqkv, P, 0, D, xT_lo.sem, xT_lo.at(a)).then_inc(q_ps.sem, 1)
                    if has(2):
                        pe.wait_ge(y_sb.sem, y_sb.at(f))
                        pe.wait_ge(xT_lo.sem, xT_lo.at(a))
                        turn(3, P, y[p]).then_inc(yT_ps.sem, 1)
                    if has(1):
                        pe.wait_ge(aT_lo.sem, aT_lo.at(f))
                        product(pe, ps[0:C, 5, 0:QKV - D], xT, wqkv, P, D, QKV, xT_lo.sem, xT_lo.at(a)).then_inc(kv_ps.sem, 1)
                    if has(0):
                        pe.wait_ge(max_sb.sem, max_sb.at(t))
                        pe.wait_ge(vT_sb.sem, vT_sb.at(t))
                        nc.tensor.transpose(ps[0:KC, 2, 0:P], negmax[p][:, :], ident[:, :]).then_inc(mt_ps.sem, 1)
                    if has(2):
                        pe.wait_ge(yT_hi.sem, yT_hi.at(f))
                        pe.wait_ge(h3_sb.sem, h3_sb.at(g))
                        product(pe, ps[0:C, 6, 0:HG], yT, w1g, P, 0, HG, yT_lo.sem, yT_lo.at(f)).then_inc(up_ps.sem, 1)
                    if has(2):
                        pe.wait_ge(h2_sb.sem, h2_sb.at(f))
                        product(pe, ps[0:C, 7, 0:HID], yT, w3s, P, 0, HID, yT_lo.sem, yT_lo.at(f)).then_inc(up_ps.sem, 1)
                    if has(1):
                        pe.wait_ge(rope_add.sem, rope_add.at(a))
                        if has(0):
                            pe.wait_ge(mrow_sb.sem, mrow_sb.at(t))
                        if has(2):
                            pe.wait_ge(yT_lo.sem, yT_lo.at(f))
                        for k in range(NH // 2 + 1):
                            last = nc.tensor.transpose(ps[:, 2 + k // 4, (k % 4) * C:(k % 4 + 1) * C],
                                                       qkr[0:C, k * P:(k + 1) * P], ident[0:C, 0:C])
                        last.then_inc(rT_ps.sem, 1)

                    def scores(i):
                        q, k = (qk_high[p], qk_low), (qk_high[p], qk_low)
                        for n_, (b, c, r) in enumerate(((0, 0, C + 1), (1, 0, C), (0, 1, C))):
                            last = nc.tensor.matmul(ps[:, i % 2, :], k[b][0:r, 1, i * P:(i + 1) * P], q[c][0:r, 0, :],
                                                    start=(n_ == 0), stop=(n_ == 2))
                        return last
                    if has(0):
                        pe.wait_ge(row_in.of(t), row_in.at(t))
                        pe.wait_ge(qk_lo.sem, qk_lo.at(t))
                        scores(0).then_inc(qk_ps.sem, 1)
                        scores(1).then_inc(qk_ps.sem, 1)
                    if has(2):
                        pe.wait_ge(gb_sb.sem, gb_sb.at(f))
                        pe.wait_ge(rope_sb.sem, rope_sb.at(a))
                        turn(4, HW, gb).then_inc(hT_ps.sem, 1)
                    if has(0):
                        for i in range(2, KC):
                            pe.wait_ge(e_sb.sem, e_sb.at(t, i - 1))
                            scores(i).then_inc(qk_ps.sem, 1)
                    if has(1):
                        pe.wait_ge(qkT_lo.sem, qkT_lo.at(a))
                        pe.wait_ge(v_sb.sem, v_sb.at(a))
                        pe.wait_ge(rope_sb.sem, rope_sb.at(a))
                        pe.wait_ge(gb_sb.sem, gb_sb.at(f))
                        for g in range(NKV):
                            r = slice(g * HD, (g + 1) * HD)
                            for i, (b, c) in enumerate(PASSES):
                                last = nc.tensor.matmul(ps[0:C, 5 + 2 * g, 0:G * C], qkT[b][r, NH // 2, :],
                                                        qkT[c][r, 0:G, :].rearrange("p a b -> p (a b)"),
                                                        start=(i == 0), stop=(i == 2))
                            last.then_inc(s_ps.sem, 1)

                    def attend(kv):
                        pe.wait_ge(qkT_lo.sem, qkT_lo.at(a))
                        pe.wait_ge(p_sb.sem, p_sb.at(a, kv + 1))
                        for j in range(G):
                            last = nc.tensor.matmul(ps[0:C, 2 + kv, j * VW:(j + 1) * VW],
                                                    prob[0:C, kv, j * C:(j + 1) * C],
                                                    vaug[a[1] % 2][0:C, kv, :], start=True, stop=True)
                        last.then_inc(pv_ps.sem, 1)
                    if has(0):
                        pe.wait_ge(vT_lo.sem, vT_lo.at(t))
                        pe.wait_ge(e_sb.sem, e_sb.at(t, 3))
                        for i in range(KC):
                            part = e_hi01 if i < 2 else e_hi23
                            pe.wait_ge(part.sem, part.at(t, i % 2 + 1))
                            for b in range(2):
                                nc.tensor.matmul(ps[0:C + 1, 0, :], vT[b][:, i, :], e_cut[0][:, i, :],
                                                 start=(i == 0 and b == 0), stop=False)
                        for i in range(KC):
                            pe.wait_ge(e_lo.sem, e_lo.at(t, i + 1))
                            last = nc.tensor.matmul(ps[0:C + 1, 0, :], vT[0][:, i, :], e_cut[1][:, i, :],
                                                    start=False, stop=(i == KC - 1))
                        last.then_inc(o_ps.sem, 1)
                    if has(1):
                        attend(0)
                    if has(2):
                        pe.wait_ge(hT_hi.sem, hT_hi.at(f))
                        pe.wait_ge(ga_sb.sem, ga_sb.at(f))
                        pe.wait_ge(ex_sb.sem, ex_sb.at(f))
                        down_part(0, 0)
                    if has(2):
                        pe.wait_ge(m16_sb.sem, m16_sb.at(f))
                        pe.wait_ge(hT_lo.sem, hT_lo.at(f))
                        nc.tensor.matmul(ps[0:C, 4, RANKS:RANKS + E], tri[0:C, 0:C], m16[0:C, :],
                                         start=True, stop=True)
                        nc.tensor.matmul(ps[:, 4, RANKS + E:RANKS + 2 * E], ones16[0:C, :], m16[0:C, :],
                                         start=True, stop=True).then_inc(rank_ps.sem, 1)
                    if has(1):
                        attend(1)
                    if has(0):
                        pe.wait_ge(hz_sb.sem, hz_sb.at(t))
                        alone(pe)
                        for i in range(KC):
                            last = nc.tensor.transpose(ps[:, 4, i * SUMS:(i + 1) * SUMS],
                                                       hz[96:C + 1, i * P:(i + 1) * P], ident[96:C + 1, 96:C + 1])
                        last.then_inc(zt_ps.sem, 1)
                    if has(2):
                        down_part(1, 0)
                each_step(pe, step)

            @block.scalar
            def _(act):
                def hi_part(dst, bank, rows):
                    return nc.scalar.activation(dst[0][0:rows, :, 0:C],
                                                ps[0:rows, bank, 0:KC * C].rearrange("p (k c) -> p k c", k=KC), ACT.Copy)

                def round_scores(b):
                    act.wait_ge(x_in.of(b), x_in.at(b))
                    act.wait_ge(qk_ps.sem, qk_ps.at(back(b, 2)))
                    nc.scalar.activation(qk_high[b[1] % 2][0:C, :, :], X[b[1] % 2][0:C, 0:2, :],
                                         ACT.Copy).then_inc(qk_hi.sem, 1)

                def step(t, has, n):
                    a, f = back(t, 1), back(t, 2)
                    p = t[1] % 2
                    if n == 0:
                        round_scores(t)
                    if has(2):
                        act.wait_ge(aT_ps.sem, aT_ps.at(f))
                        act.wait_ge(wo_ps.sem, wo_ps.at(back(f, 1)))
                        hi_part(aT, 5, P).then_inc(aT_hi.sem, 1)
                    if has(0):
                        act.wait_ge(vT_ps.sem, vT_ps.at(t))
                        act.wait_ge(vT_lo.sem, vT_lo.at(a))
                        nc.scalar.activation(vT_full[:, :, :], ps[:, 2, 0:KC * C].rearrange("p (k c) -> p k c", k=KC),
                                             ACT.Copy).then_inc(vT_sb.sem, 1)
                        act.wait_ge(vT_sb.sem, vT_sb.at(t))
                        act.wait_ge(o_ps.sem, o_ps.at(a))
                        nc.scalar.activation(vT[0][:, :, 0:C], vT_full[:, :, :], ACT.Copy).then_inc(vT_hi.sem, 1)
                    if has(1):
                        act.wait_ge(xT_ps.sem, xT_ps.at(a))
                        act.wait_ge(kv_ps.sem, kv_ps.at(f))
                        hi_part(xT, 3, P).then_inc(xT_hi.sem, 1)
                    if has(2):
                        act.wait_ge(yT_ps.sem, yT_ps.at(f))
                        act.wait_ge(up_ps.sem, up_ps.at(back(f, 1)))
                        hi_part(yT, 3, P).then_inc(yT_hi.sem, 1)
                    if has(1):
                        act.wait_ge(kv_ps.sem, kv_ps.at(a))
                        act.wait_ge(pv_ps.sem, pv_ps.at(back(a, 2)))
                        nc.scalar.activation(vaug[a[1] % 2][0:C, :, 0:HD], ps[0:C, 5, QK - D:QKV - D].rearrange(
                            "p (g d) -> p g d", g=NKV), ACT.Copy).then_inc(v_sb.sem, 1)
                    if has(2):
                        act.wait_ge(up_ps.sem, up_ps.at(f, 1))
                        act.wait_ge(ga_sb.sem, ga_sb.at(back(f, 1)))
                        nc.scalar.activation(th[0:C, :], ps[0:C, 6, 0:HID], ACT.Tanh, scale=0.5).then_inc(th_sb.sem, 1)
                        act.wait_ge(nl_sb.sem, nl_sb.at(f))
                        act.wait_ge(pick.sem, pick.at(back(f, 1)))
                        nc.scalar.activation(ex[0:C, :], ps[0:C, 6, HID:HG], ACT.Exp, bias=nl[0:C, :],
                                             accum_out=se[0:C, :]).then_inc(ex_sb.sem, 1)

                    if has(-1):
                        round_scores(back(t, -1))

                    def weights(i):
                        act.wait_ge(qk_ps.sem, qk_ps.at(t, i + 1))
                        act.wait_ge(e_lo.sem, e_lo.at(a, i + 1))
                        nc.scalar.activation(e[:, i, :], ps[:, i % 2, :], ACT.Exp, scale=QS).then_inc(e_sb.sem, 1)

                    def weights_hi(i):
                        act.wait_ge(e_sb.sem, e_sb.at(t, i + 1))
                        act.wait_ge(o_ps.sem, o_ps.at(a))
                        nc.scalar.activation(e_cut[0][:, i, :], e[:, i, :], ACT.Copy).then_inc(e_hi23.sem, 1)
                    if has(1):
                        act.wait_ge(rT_ps.sem, rT_ps.at(a))
                        act.wait_ge(s_ps.sem, s_ps.at(f))
                        nc.scalar.activation(qkT[0][:, 0:4, :], ps[:, 2, 0:4 * C].rearrange("p (k c) -> p k c", k=4),
                                             ACT.Copy)
                        nc.scalar.activation(qkT[0][:, 4, :], ps[:, 3, 0:C], ACT.Copy).then_inc(qkT_hi.sem, 1)
                    if has(0):
                        weights(0)
                        weights(1)
                    if has(0):
                        weights(2)
                        weights(3)
                        weights_hi(2)
                        weights_hi(3)
                    if has(2):
                        act.wait_ge(hT_ps.sem, hT_ps.at(f))
                        act.wait_ge(dn_ps.sem, dn_ps.at(back(f, 1)))
                        hi_part(hT, 4, HW).then_inc(hT_hi.sem, 1)
                    if has(1):
                        for g in range(NKV):
                            act.wait_ge(s_ps.sem, s_ps.at(a, g + 1))
                            act.wait_ge(p_sb.sem, p_sb.at(a, g) if g else p_sb.at(f))
                            nc.scalar.activation(capped[0:C, :], ps[0:C, 5 + 2 * g, 0:G * C], ACT.Tanh,
                                                 scale=TANH).then_inc(tanh_sb.sem, 1)
                            act.wait_ge(tanh_sb.sem, tanh_sb.at(a, g + 1))
                            act.wait_ge(pv_ps.sem, pv_ps.at(f))
                            nc.scalar.activation(prob[0:C, g, :], capped[0:C, :], ACT.Exp,
                                                 scale=CAPF).then_inc(p_sb.sem, 1)
                    if has(0):
                        act.wait_ge(o_ps.sem, o_ps.at(t))
                        act.wait_ge(h_sb.sem, h_sb.at(a))
                        act.wait_ge(zt_ps.sem, zt_ps.at(a))
                        nc.scalar.activation(hz[0:C + 1, :], ps[0:C + 1, 0, :], ACT.Copy).then_inc(hz_sb.sem, 1)
                each_step(act, step)

            @block.vector
            def _(dve):
                def lo_part(dst, bank, rows):
                    return nc.vector.tensor_tensor(dst[1][0:rows, :, 0:C],
                                                   ps[0:rows, bank, 0:KC * C].rearrange("p (k c) -> p k c", k=KC),
                                                   dst[0][0:rows, :, 0:C].bitcast(F32), ALU.subtract)

                def step(t, has, n):
                    a, f, g = back(t, 1), back(t, 2), back(t, 3)
                    p, pa = t[1] % 2, a[1] % 2
                    if has(1):
                        dve.wait_ge(rzT_ps.sem, rzT_ps.at(a))
                        dve.wait_ge(bc_ps.sem, bc_ps.at(f))
                        nc.vector.tensor_copy(rzT[0:KC, :], ps[0:KC, 4, KC * SUMS:KC * SUMS + P]).then_inc(rzT_sb.sem, 1)

                    def maxima(i):
                        dve.wait_ge(mx_ps.sem, mx_ps.at(t, i + 1))
                        nc.vector.tensor_reduce(negmax[p][:, i:i + 1], ps[:, i % 2, :], AX.X, ALU.max,
                                                negate=True).then_inc(max_sb.sem, 1)
                    if has(0):
                        dve.wait_ge(mt_ps.sem, mt_ps.at(f))
                        maxima(0)
                        maxima(1)
                    if has(1):
                        dve.wait_ge(bc_ps.sem, bc_ps.at(a))
                        dve.wait_ge(hz_sb.sem, hz_sb.at(a))
                        nc.vector.tensor_tensor(h[pa][0:C, :], ps[0:C, 7, :], hz[0:C, :],
                                                ALU.mult).then_inc(h_sb.sem, 1)
                        dve.wait_ge(h_sb.sem, h_sb.at(a))
                        nc.vector.bn_stats(st1[0:C, :], h[pa][0:C, :]).then_inc(st1_sb.sem, 1)
                        dve.wait_ge(st1_sb.sem, st1_sb.at(a))
                        alone(dve)
                        nc.vector.bn_aggr(ag1[0:C, :], st1[0:C, :]).then_inc(ag1_sb.sem, 1)
                    if has(2):
                        dve.wait_ge(aT_hi.sem, aT_hi.at(f))
                        lo_part(aT, 5, P).then_inc(aT_lo.sem, 1)
                    if has(1):
                        dve.wait_ge(rs1_sb.sem, rs1_sb.at(a))
                        dve.wait_ge(xT_ps.sem, xT_ps.at(f))
                        nc.vector.tensor_scalar(xn[0:C, :], h[pa][0:C, :], ag1[0:C, 0:1], rs1[0:C, :],
                                                ALU.subtract, ALU.mult).then_inc(xn_sb.sem, 1)
                    if has(3):
                        c2 = [0]

                        def placed(ins):
                            ins.then_inc(place.sem, 1)
                            c2[0] += 1
                            dve.wait_ge(place.sem, place.at(g, c2[0]))
                        dve.wait_ge(rank_ps.sem, rank_ps.at(g))
                        placed(nc.vector.tensor_tensor(posb[0:C, :], ps[0:C, 4, RANKS:RANKS + E], base[0:C, :], ALU.add))
                        placed(nc.vector.tensor_tensor(base[:, :], ps[:, 4, RANKS + E:RANKS + 2 * E], base[:, :], ALU.add))
                        for k in range(2):
                            placed(nc.vector.scalar_tensor_tensor(junk[0:C, :], posb[0:C, :], 1.0, oh[0:C, k, :],
                                                                  ALU.mult, ALU.mult, accum_out=slotf[0:C, k:k + 1]))
                        placed(nc.vector.tensor_copy(slot[g[1] % 2][0:C, :], slotf[0:C, :]))
                    if has(2):
                        dve.wait_ge(wo_ps.sem, wo_ps.at(f))
                        nc.vector.tensor_tensor(h2[p][0:C, :], ps[0:C, 7, :], h[p][0:C, :],
                                                ALU.add).then_inc(h2_sb.sem, 1)
                        dve.wait_ge(h2_sb.sem, h2_sb.at(f))
                        nc.vector.bn_stats(st2[0:C, :], h2[p][0:C, :]).then_inc(st2_sb.sem, 1)
                        dve.wait_ge(st2_sb.sem, st2_sb.at(f))
                        dve.wait_ge(y_sb.sem, y_sb.at(back(f, 1)))
                        alone(dve)
                        nc.vector.bn_aggr(ag2[0:C, :], st2[0:C, :]).then_inc(ag2_sb.sem, 1)
                    if has(1):
                        dve.wait_ge(xT_hi.sem, xT_hi.at(a))
                        lo_part(xT, 3, P).then_inc(xT_lo.sem, 1)
                    if has(2):
                        dve.wait_ge(rs2_sb.sem, rs2_sb.at(f))
                        dve.wait_ge(y_out.of(back(f, 2)), y_out.at(back(f, 2)))
                        nc.vector.tensor_scalar(y[p][0:C, :], h2[p][0:C, :], ag2[0:C, 0:1], rs2[0:C, :],
                                                ALU.subtract, ALU.mult).then_inc(y_sb.sem, 1)
                    if has(0):
                        maxima(2)
                        maxima(3)
                    if has(3):
                        dve.wait_ge(dn_ps.sem, dn_ps.at(g))
                        dve.wait_ge(h3_out.of(back(g, 2)), h3_out.at(back(g, 2)))
                        nc.vector.tensor_tensor(h3[g[1] % 2][0:C, :], ps[0:C, 6, :], h2[g[1] % 2][0:C, :],
                                                ALU.add).then_inc(h3_sb.sem, 1)
                    if has(2):
                        dve.wait_ge(yT_hi.sem, yT_hi.at(f))
                        lo_part(yT, 3, P).then_inc(yT_lo.sem, 1)
                    if has(1):
                        dve.wait_ge(rope_add.sem, rope_add.at(f))
                        dve.wait_ge(v_sb.sem, v_sb.at(a))
                        heads = QK // HD
                        flat = ps[0:C, 4:6, :].rearrange("p a b -> p (a b)")[:, 0:QK]
                        halves = flat.rearrange("p (h s d) -> p h s d", h=heads, s=2)
                        nc.vector.tensor_tensor(rc[0:C, :].rearrange("p (h d) -> p h d", h=heads),
                                                flat.rearrange("p (h d) -> p h d", h=heads),
                                                cos_t[0:C, None, :].to_broadcast([C, heads, HD]),
                                                ALU.mult).then_inc(rope_sb.sem, 1)
                        turned = rsn[0:C, :].rearrange("p (h s d) -> p h s d", h=heads, s=2)
                        for s in range(2):
                            sines = sin_t[0:C, None, s * (HD // 2):(s + 1) * (HD // 2)]
                            nc.vector.tensor_tensor(turned[:, :, s, :], halves[:, :, 1 - s, :],
                                                    sines.to_broadcast([C, heads, HD // 2]),
                                                    ALU.mult).then_inc(rope_sb.sem, 1)
                    if has(0):
                        dve.wait_ge(mt_ps.sem, mt_ps.at(t))
                        dve.wait_ge(row_in.of(f), row_in.at(f))
                        nc.vector.tensor_copy(mrow[p][:, :], ps[0:KC, 2, 0:P]).then_inc(mrow_sb.sem, 1)
                    if has(2):
                        dve.wait_ge(th_sb.sem, th_sb.at(f))
                        dve.wait_ge(pick.sem, pick.at(back(f, 1)))
                        nc.vector.tensor_reduce(nl[0:C, :], ps[0:C, 6, HID:HG], AX.X, ALU.max,
                                                negate=True).then_inc(nl_sb.sem, 1)
                        dve.wait_ge(ex_sb.sem, ex_sb.at(f))
                        nc.vector.scalar_tensor_tensor(ga[0:C, :], th[0:C, :], 1.0, ps[0:C, 6, 0:HID],
                                                       ALU.add, ALU.mult).then_inc(ga_sb.sem, 1)
                        dve.wait_ge(ga_sb.sem, ga_sb.at(f))
                        dve.wait_ge(up_ps.sem, up_ps.at(f))
                        dve.wait_ge(hT_ps.sem, hT_ps.at(back(f, 1)))
                        nc.vector.scalar_tensor_tensor(gb[0:C, :], ga[0:C, :], 0.5, ps[0:C, 7, 0:HID],
                                                       ALU.mult, ALU.mult).then_inc(gb_sb.sem, 1)
                    if has(1):
                        dve.wait_ge(qkT_hi.sem, qkT_hi.at(a))
                        nc.vector.tensor_tensor(qkT[1][:, 0:4, :], ps[:, 2, 0:4 * C].rearrange("p (k c) -> p k c", k=4),
                                                qkT[0][:, 0:4, :].bitcast(F32), ALU.subtract)
                        nc.vector.tensor_tensor(qkT[1][:, 4, :], ps[:, 3, 0:C], qkT[0][:, 4, :].bitcast(F32),
                                                ALU.subtract).then_inc(qkT_lo.sem, 1)
                    if has(0):
                        dve.wait_ge(o_ps.sem, o_ps.at(a))
                        for i in range(2):
                            dve.wait_ge(e_sb.sem, e_sb.at(t, i + 1))
                            nc.vector.tensor_copy(e_cut[0][:, i, :], e[:, i, :]).then_inc(e_hi01.sem, 1)
                            dve.wait_ge(e_hi01.sem, e_hi01.at(t, i + 1))
                            nc.vector.tensor_tensor(e_cut[1][:, i, :], e[:, i, :], e_cut[0][:, i, :].bitcast(F32),
                                                    ALU.subtract).then_inc(e_lo.sem, 1)
                    if has(2):
                        c = [0]

                        def chosen(ins):
                            ins.then_inc(pick.sem, 1)
                            c[0] += 1
                            dve.wait_ge(pick.sem, pick.at(f, c[0]))
                        dve.wait_ge(place.sem, place.at(back(f, 1)))
                        chosen(nc.vector.reciprocal(rse[0:C, :], se[0:C, :]))
                        chosen(nc.vector.tensor_scalar(sc[0:C, :], ex[0:C, :], rse[0:C, :], None, ALU.mult))
                        chosen(nc.vector.tensor_tensor(met[0:C, :], sc[0:C, :], bias_t[0:C, :], ALU.add))
                    if has(0):
                        for i in range(2, KC):
                            dve.wait_ge(e_hi23.sem, e_hi23.at(t, i - 1))
                            nc.vector.tensor_tensor(e_cut[1][:, i, :], e[:, i, :], e_cut[0][:, i, :].bitcast(F32),
                                                    ALU.subtract).then_inc(e_lo.sem, 1)
                    if has(2):
                        alone(dve)
                        chosen(nc.vector.max(v8[0:C, :], met[0:C, :]))
                        alone(dve)
                        chosen(nc.vector.max_index(i8[0:C, :], v8[0:C, :], met[0:C, :]))
                        chosen(nc.vector.tensor_copy(i2[0:C, :], i8[0:C, 0:2]))
                        for k in range(2):
                            chosen(nc.vector.tensor_scalar(oh[0:C, k, :], iota8[0:C, :], i2[0:C, k:k + 1], None,
                                                           ALU.is_equal))
                        dve.wait_ge(rank_ps.sem, rank_ps.at(back(f, 1)))
                        nc.vector.tensor_tensor(m16[0:C, :], oh[0:C, 0, :], oh[0:C, 1, :],
                                                ALU.add).then_inc(m16_sb.sem, 1)
                    if has(2):
                        dve.wait_ge(hT_hi.sem, hT_hi.at(f))
                        lo_part(hT, 4, HW).then_inc(hT_lo.sem, 1)
                        dve.wait_ge(scattered.of(back(f, 2)), scattered.at(back(f, 2)))
                        for k in range(2):
                            chosen(nc.vector.scalar_tensor_tensor(junk[0:C, :], sc[0:C, :], 1.0, oh[0:C, k, :],
                                                                  ALU.mult, ALU.mult, accum_out=entry[k][p][0:C, 1:2]))
                        chosen(nc.vector.tensor_scalar(tokf[:], tokf[:], float(C), None, ALU.add))
                        for k in range(2):
                            last = nc.vector.tensor_copy(entry[k][p][0:C, 0:1].bitcast(I32), tokf[0:C, :])
                        chosen(last)

                    def normalise(kv):
                        dve.wait_ge(pv_ps.sem, pv_ps.at(a, kv + 1))
                        av = ps[0:C, 2 + kv, 0:G * VW].rearrange("p (j d) -> p j d", j=G)
                        rd_v = rden[0:C, kv * G:(kv + 1) * G]
                        nc.vector.reciprocal(rd_v, av[:, :, HD]).then_inc(rden_sb.sem, 1)
                        dve.wait_ge(rden_sb.sem, rden_sb.at(a, kv + 1))
                        dve.wait_ge(aT_ps.sem, aT_ps.at(f))
                        nc.vector.tensor_tensor(attn[0:C, kv * G:(kv + 1) * G, :], av[:, :, 0:HD],
                                                rd_v[:, :, None].to_broadcast([C, G, HD]),
                                                ALU.mult).then_inc(attn_sb.sem, 1)
                    if has(1):
                        normalise(0)
                    if has(0):
                        dve.wait_ge(zt_ps.sem, zt_ps.at(t))
                        nc.vector.reciprocal(rz[:, :], ps[:, 4, 0:KC * SUMS].rearrange(
                            "p (k w) -> p k w", k=KC)[:, :, SUMS - 1]).then_inc(rz_sb.sem, 1)
                    if has(1):
                        normalise(1)
                each_step(dve, step)

            @block.gpsimd
            def _(pool):
                last_entry = pool.to_reg(REGIONS - 1)

                def rstd(b, aggr, ve, rs, aggr_sb, ve_done, rs_done, rs_used):
                    pool.wait_ge(aggr_sb.sem, aggr_sb.at(b))
                    pool.wait_ge(rs_used.sem, rs_used.at(back(b, 1)))
                    alone(pool)
                    nc.gpsimd.tensor_scalar(ve[0:C, :], aggr[0:C, 1:2], EPS, None, ALU.add).then_inc(ve_done.sem, 1)
                    pool.wait_ge(ve_done.sem, ve_done.at(b))
                    alone(pool)
                    nc.gpsimd.tensor_tensor(out=rs[0:C, :], in0=ve[0:C, :], in1=mhalf[0:C, :],
                                            op=ALU.pow).then_inc(rs_done.sem, 1)

                def cut_scores(b):
                    q = b[1] % 2
                    pool.wait_ge(qk_hi.sem, qk_hi.at(b))
                    pool.wait_ge(qk_ps.sem, qk_ps.at(back(b, 1)))
                    alone(pool)
                    nc.gpsimd.tensor_tensor(out=qk_low[0:C, :, :], in0=X[q][0:C, 0:2, :],
                                            in1=qk_high[q][0:C, :, :].bitcast(F32),
                                            op=ALU.subtract).then_inc(qk_lo.sem, 1)

                def step(t, has, n):
                    a, f, g = back(t, 1), back(t, 2), back(t, 3)
                    if n == 0:
                        cut_scores(t)
                    if has(1):
                        rstd(a, ag1, ve1, rs1, ag1_sb, ve1_sb, rs1_sb, xn_sb)
                    if has(0):
                        pool.wait_ge(vT_hi.sem, vT_hi.at(t))
                        pool.wait_ge(o_ps.sem, o_ps.at(a))
                        alone(pool)
                        nc.gpsimd.tensor_tensor(out=vT[1][:, :, 0:C], in0=vT_full[:, :, :],
                                                in1=vT[0][:, :, 0:C].bitcast(F32),
                                                op=ALU.subtract).then_inc(vT_lo.sem, 1)
                    if has(2):
                        rstd(f, ag2, ve2, rs2, ag2_sb, ve2_sb, rs2_sb, y_sb)
                    if has(3):
                        pool.wait_ge(pick.sem, pick.at(g))
                        pool.wait_ge(place.sem, place.at(g))
                        alone(pool)
                        for k in range(2):
                            nc.gpsimd.indirect_dma_start(
                                routed, bass.IndirectOffsetOnAxis(ap=slot[g[1] % 2][0:C, k:k + 1], axis=0),
                                entry[k][g[1] % 2][0:C, :], None, bounds_check=last_entry,
                                oob_is_err=False).then_inc(scattered.of(g), 16)
                    if has(1):
                        pool.wait_ge(rope_sb.sem, rope_sb.at(a))
                        pool.wait_ge(rT_ps.sem, rT_ps.at(f))
                        alone(pool)
                        nc.gpsimd.tensor_tensor(out=qkr[0:C, :], in0=rc[0:C, :], in1=rsn[0:C, :],
                                                op=ALU.add).then_inc(rope_add.sem, 1)
                    if has(-1):
                        cut_scores(back(t, -1))
                each_step(pool, step)
                for b in ((0, NB - 2), (0, NB - 1)):
                    pool.wait_ge(scattered.of(b), scattered.at(b))

        tower.close()

        group_row = sbuf("group_row", [1, NG], I32)
        group_expert = sbuf("group_expert", [1, NG], I32)
        with ExitStack() as c1:
            groups = sbuf("groups", [1, E], F32, c1)
            groups_i = sbuf("groups_i", [1, E], I32, c1)
            upto = sbuf("upto", [1, E], F32, c1)
            skip = sbuf("skip", [1, E], F32, c1)
            number = sbuf("number", [1, NG], F32, c1)
            expert_f = sbuf("expert_f", [1, NG], F32, c1)
            row_f = sbuf("row_f", [1, NG], F32, c1)
            passed = sbuf("passed", [1, NG], F32, c1)
            p_iota, p_dve = (c1.enter_context(nc.semaphore(n)) for n in ("p_iota", "p_dve"))
            with nc.Block() as block:
                @block.gpsimd
                def _(pool):
                    nc.gpsimd.iota(number[:], [[1, NG]], base=0, channel_multiplier=0,
                                   allow_small_or_imprecise_dtypes=True).then_inc(p_iota, 1)
                    nc.gpsimd.iota(skip[:], [[CAP, E]], base=0, channel_multiplier=0,
                                   allow_small_or_imprecise_dtypes=True).then_inc(p_iota, 1)

                @block.vector
                def _(dve):
                    done = [0]

                    def then(ins):
                        ins.then_inc(p_dve, 1)
                        done[0] += 1
                        dve.wait_ge(p_dve, done[0])
                    dve.wait_ge(p_iota, 2)
                    then(nc.vector.tensor_tensor(groups[:], base[0:1, :], skip[:], ALU.subtract))
                    then(nc.vector.tensor_scalar(groups[:], groups[:], float(GROUP - 1), None, ALU.add))
                    then(nc.vector.tensor_copy(groups_i[:], groups[:]))
                    then(nc.vector.tensor_scalar(groups_i[:], groups_i[:], GROUP.bit_length() - 1, None,
                                                 ALU.logical_shift_right))
                    then(nc.vector.tensor_copy(groups[:], groups_i[:]))
                    then(nc.vector.tensor_copy(upto[:, 0:1], groups[:, 0:1]))
                    for i in range(1, E):
                        then(nc.vector.tensor_tensor(upto[:, i:i + 1], upto[:, i - 1:i], groups[:, i:i + 1], ALU.add))
                    then(nc.vector.tensor_scalar(skip[:], groups[:], -float(GROUP), float(CAP), ALU.mult, ALU.add))
                    then(nc.vector.tensor_scalar(row_f[:], number[:], float(GROUP), None, ALU.mult))
                    then(nc.vector.memset(expert_f[:], 0.0))
                    for i in range(E):
                        then(nc.vector.tensor_scalar(passed[:], number[:], upto[:, i:i + 1], None, ALU.is_ge))
                        then(nc.vector.tensor_tensor(expert_f[:], expert_f[:], passed[:], ALU.add))
                        then(nc.vector.scalar_tensor_tensor(row_f[:], passed[:], skip[:, i:i + 1], row_f[:],
                                                            ALU.mult, ALU.add))
                    then(nc.vector.tensor_scalar(expert_f[:], expert_f[:], float(E - 1), None, ALU.min))
                    then(nc.vector.tensor_scalar(row_f[:], row_f[:], float(E * CAP), None, ALU.min))
                    then(nc.vector.tensor_copy(group_expert[:], expert_f[:]))
                    then(nc.vector.tensor_copy(group_row[:], row_f[:]))

        with ExitStack() as c2:
            def pair(name, shape, dt=F32):
                return [sbuf(f"{name}{p}", shape, dt, c2) for p in range(2)]

            raw1 = sbuf("raw1", [P, KC, HID], F32, c2)
            raw3 = sbuf("raw3", [P, KC, HID], F32, c2)
            raw2 = sbuf("raw2", [HW, HC, D], F32, c2)
            raws = (raw1, raw3, raw2)
            W = [tuple((sbuf(f"e{n}_hi{p}", r.shape, F32R, c2), sbuf(f"e{n}_lo{p}", r.shape, F32R, c2))
                       for n, r in enumerate(raws)) for p in range(2)]
            entries = pair("entries", [P, GROUP_TILES, ENTRY])
            rows, scaled = pair("rows", [P, D]), pair("scaled", [P, D])
            rT = pair("rT_hi", [P, KC, P], F32R), pair("rT_lo", [P, KC, P], F32R)
            th, ga = sbuf("eth", [P, HID], F32, c2), sbuf("ega", [P, HID], F32, c2)
            gb = pair("egb", [P, HID])
            uT = (sbuf("uT_hi", [HW, HC, P], F32R, c2), sbuf("uT_lo", [HW, HC, P], F32R, c2))
            res = pair("res", [P, D])

            def tiles(name, per=1):
                return Signal(c2.enter_context(nc.semaphore(name)), per)

            def pair_of(name):
                return DmaSignal(*(c2.enter_context(nc.semaphore(f"{name}_{p}")) for p in range(2)))

            entries_in, rows_in = pair_of("entries_in"), pair_of("rows_in")
            w_in = [pair_of(f"w_in{n}") for n in range(3)]
            added = tiles("added", 16)
            rT_ps, u_ps, uT_ps, d_ps = tiles("t_rT_ps"), tiles("t_u_ps", 2), tiles("t_uT_ps"), tiles("t_d_ps")
            scaled_sb, rT_hi, th_sb, uT_hi = (tiles("t_" + n) for n in ("scaled_sb", "rT_hi", "th_sb", "uT_hi"))
            rT_lo, ga_sb, gb_sb, uT_lo, res_sb = (tiles("t_" + n) for n in ("rT_lo", "ga_sb", "gb_sb", "uT_lo", "res_sb"))
            w_hi, w_lo = [tiles(f"w_hi{n}") for n in range(3)], [tiles(f"w_lo{n}") for n in range(3)]
            cleared = c2.enter_context(nc.semaphore("cleared"))

            T = GROUP_TILES

            def tile_of(group, i):
                j, off = group
                return (T * j, T * off + i)

            def each_group(eng, work):
                work((0, 0), True, False)
                work((0, 1), False, False)
                with eng.Fori(1, NG // 2 - 1) as j:
                    work((j, 0), False, False)
                    work((j, 1), False, False)
                work((0, NG - 2), False, False)
                work((0, NG - 1), False, True)

            with nc.Block() as block:
                @block.sync
                def _(sp):
                    def at(table, group):
                        n = 2 * group[0] + group[1]
                        return table[0:1, n:n + 1] if isinstance(n, int) else table[0:1, bass.ds(n, 1)]

                    def fetch(group):
                        ex = sp.value_load(at(group_expert, group), min_val=0, max_val=E - 1)
                        for n, (src, pp) in enumerate(((w1, P), (w3, P), (w2, HW))):
                            sp.wait_ge(w_lo[n].sem, w_lo[n].at(back(group, 1)))
                            alone(sp)
                            sp.dma_start(raws[n][:], src[bass.ds(ex, 1)].rearrange(
                                "o (k p) h -> p (o k) h", p=pp)).then_inc(w_in[n].of(group), 16)
                        sp.wait_ge(added.sem, added.at(tile_of(back(group, 2), T - 1)))
                        alone(sp)
                        row = sp.value_load(at(group_row, group), min_val=0, max_val=E * CAP)
                        sp.dma_start(entries[group[1] % 2][:], routed[bass.ds(row, GROUP), :].rearrange(
                            "(p i) c -> p i c", p=P)).then_inc(entries_in.of(group), 16)

                    def work(group, first, last):
                        if first:
                            fetch(group)
                        if not last:
                            fetch(back(group, -1))
                    each_group(sp, work)

                @block.tensor
                def _(pe):
                    def cut(dst, lhs, rhs, width, rows_, lo, at):
                        for i, (a, b) in enumerate(PASSES):
                            if i == 2:
                                pe.wait_ge(lo, at)
                            for k in range(KC):
                                ins = nc.tensor.matmul(dst, lhs[a][:rows_, k, :], rhs[b][:rows_, k, 0:width],
                                                       start=(k == 0 and i == 0), stop=(k == KC - 1 and i == 2))
                        return ins

                    def turn_rows(group, i):
                        t = tile_of(group, i)
                        pe.wait_ge(scaled_sb.sem, scaled_sb.at(t))
                        pe.wait_ge(rT_lo.sem, rT_lo.at(back(t, 2)))
                        for k in range(KC):
                            last = nc.tensor.transpose(ps[:, i % 2, k * P:(k + 1) * P],
                                                       scaled[i % 2][:, k * P:(k + 1) * P], ident[:])
                        last.then_inc(rT_ps.sem, 1)

                    def turn_hidden(group, i):
                        t = tile_of(group, i)
                        pe.wait_ge(gb_sb.sem, gb_sb.at(t))
                        pe.wait_ge(uT_lo.sem, uT_lo.at(back(t, 1)))
                        for k in range(HC):
                            last = nc.tensor.transpose(ps[0:HW, 6, k * P:(k + 1) * P],
                                                       gb[i % 2][:, k * HW:(k + 1) * HW], ident[:])
                        last.then_inc(uT_ps.sem, 1)

                    def down(group, i):
                        t = tile_of(group, i)
                        pe.wait_ge(uT_hi.sem, uT_hi.at(t))
                        if i == 0:
                            pe.wait_ge(w_lo[2].sem, w_lo[2].at(group))
                        pe.wait_ge(res_sb.sem, res_sb.at(back(t, 1)))
                        cut(ps[:, 7, :], uT, W[group[1] % 2][2], D, HW, uT_lo.sem, uT_lo.at(t)).then_inc(d_ps.sem, 1)

                    def work(group, first, last):
                        q = group[1] % 2
                        if first:
                            turn_rows(group, 0)
                        for i in range(T):
                            t = tile_of(group, i)
                            before = (group, i - 1) if i > 0 else (back(group, 1), T - 1)
                            if i == T - 1 and not last:
                                turn_rows(back(group, -1), 0)
                            elif i < T - 1:
                                turn_rows(group, i + 1)
                            if i == 0:
                                pe.wait_ge(w_lo[0].sem, w_lo[0].at(group))
                                pe.wait_ge(w_lo[1].sem, w_lo[1].at(group))
                            pe.wait_ge(rT_hi.sem, rT_hi.at(t))
                            b = 2 + 2 * (i % 2)
                            pe.wait_ge(ga_sb.sem, ga_sb.at(back(t, 2)))
                            lhs = (rT[0][i % 2], rT[1][i % 2])
                            cut(ps[:, b, 0:HID], lhs, W[q][0], HID, P, rT_lo.sem, rT_lo.at(t)).then_inc(u_ps.sem, 1)
                            if not (first and i == 0):
                                turn_hidden(*before)
                            pe.wait_ge(gb_sb.sem, gb_sb.at(back(t, 2)))
                            cut(ps[:, b + 1, 0:HID], lhs, W[q][1], HID, P, rT_lo.sem, rT_lo.at(t)).then_inc(u_ps.sem, 1)
                            if not (first and i == 0):
                                down(*before)
                        if last:
                            turn_hidden(group, T - 1)
                            down(group, T - 1)
                    each_group(pe, work)

                @block.scalar
                def _(act):
                    def cut_weight(group, n):
                        act.wait_ge(w_in[n].of(group), w_in[n].at(group))
                        used = d_ps if n == 2 else u_ps
                        act.wait_ge(used.sem, used.at(tile_of(back(group, 2), T - 1)))
                        nc.scalar.activation(W[group[1] % 2][n][0][:], raws[n][:], ACT.Copy).then_inc(w_hi[n].sem, 1)

                    def scale_rows(group, i):
                        t = tile_of(group, i)
                        act.wait_ge(rows_in.of(t), rows_in.at(t))
                        act.wait_ge(rT_ps.sem, rT_ps.at(back(t, 2)))
                        nc.scalar.activation(scaled[i % 2][:], rows[i % 2][:], ACT.Copy,
                                                            scale=entries[group[1] % 2][:, i, 1:2]).then_inc(scaled_sb.sem, 1)

                    def rows_hi(t, i):
                        act.wait_ge(rT_ps.sem, rT_ps.at(t))
                        act.wait_ge(u_ps.sem, u_ps.at(back(t, 2)))
                        nc.scalar.activation(rT[0][i % 2][:], ps[:, i % 2, :].rearrange(
                            "p (k c) -> p k c", k=KC), ACT.Copy).then_inc(rT_hi.sem, 1)

                    def hidden_hi(t):
                        act.wait_ge(uT_ps.sem, uT_ps.at(t))
                        act.wait_ge(d_ps.sem, d_ps.at(back(t, 1)))
                        nc.scalar.activation(uT[0][:], ps[0:HW, 6, :].rearrange(
                            "p (k c) -> p k c", k=HC), ACT.Copy).then_inc(uT_hi.sem, 1)

                    def work(group, first, last):
                        if first:
                            scale_rows(group, 0)
                            scale_rows(group, 1)
                            for n in range(3):
                                cut_weight(group, n)
                            rows_hi(tile_of(group, 0), 0)
                        for i in range(T):
                            t = tile_of(group, i)
                            if not (last and i == T - 1):
                                rows_hi(back(t, -1), i + 1)
                            act.wait_ge(u_ps.sem, u_ps.at(t, 1))
                            act.wait_ge(ga_sb.sem, ga_sb.at(back(t, 1)))
                            nc.scalar.activation(th[:], ps[:, 2 + 2 * (i % 2), 0:HID], ACT.Tanh, scale=0.5).then_inc(th_sb.sem, 1)
                            if not (first and i == 0):
                                hidden_hi(back(t, 1))
                            if i < T - 2:
                                scale_rows(group, i + 2)
                            elif not last:
                                scale_rows(back(group, -1), i + 2 - T)
                            if i < 3 and not last:
                                cut_weight(back(group, -1), i)
                        if last:
                            hidden_hi(tile_of(group, T - 1))
                    each_group(act, work)

                @block.vector
                def _(dve):
                    for p in range(2):
                        nc.vector.memset(rows[p][:], 0.0).then_inc(cleared, 1)

                    def cut_weight(group, n):
                        dve.wait_ge(w_hi[n].sem, w_hi[n].at(group))
                        nc.vector.tensor_tensor(W[group[1] % 2][n][1][:], raws[n][:],
                                                             W[group[1] % 2][n][0][:].bitcast(F32), ALU.subtract).then_inc(w_lo[n].sem, 1)

                    def rows_lo(t, i):
                        dve.wait_ge(rT_hi.sem, rT_hi.at(t))
                        dve.wait_ge(u_ps.sem, u_ps.at(back(t, 2)))
                        nc.vector.tensor_tensor(rT[1][i % 2][:], ps[:, i % 2, :].rearrange(
                            "p (k c) -> p k c", k=KC), rT[0][i % 2][:].bitcast(F32), ALU.subtract).then_inc(rT_lo.sem, 1)

                    def hidden_lo(t):
                        dve.wait_ge(uT_hi.sem, uT_hi.at(t))
                        dve.wait_ge(d_ps.sem, d_ps.at(back(t, 1)))
                        nc.vector.tensor_tensor(uT[1][:], ps[0:HW, 6, :].rearrange(
                            "p (k c) -> p k c", k=HC), uT[0][:].bitcast(F32), ALU.subtract).then_inc(uT_lo.sem, 1)

                    def result(t, i):
                        dve.wait_ge(d_ps.sem, d_ps.at(t))
                        dve.wait_ge(added.sem, added.at(back(t, 2)))
                        nc.vector.tensor_copy(res[i % 2][:], ps[:, 7, :]).then_inc(res_sb.sem, 1)

                    def work(group, first, last):
                        if first:
                            cut_weight(group, 2)
                            rows_lo(tile_of(group, 0), 0)
                        for i in range(T):
                            t = tile_of(group, i)
                            if not (last and i == T - 1):
                                rows_lo(back(t, -1), i + 1)
                            dve.wait_ge(th_sb.sem, th_sb.at(t))
                            dve.wait_ge(gb_sb.sem, gb_sb.at(back(t, 1)))
                            b = 2 + 2 * (i % 2)
                            nc.vector.scalar_tensor_tensor(ga[:], th[:], 1.0, ps[:, b, 0:HID],
                                                                      ALU.add, ALU.mult).then_inc(ga_sb.sem, 1)
                            if not (first and i == 0):
                                hidden_lo(back(t, 1))
                            dve.wait_ge(ga_sb.sem, ga_sb.at(t))
                            dve.wait_ge(u_ps.sem, u_ps.at(t))
                            dve.wait_ge(uT_ps.sem, uT_ps.at(back(t, 2)))
                            nc.vector.scalar_tensor_tensor(gb[i % 2][:], ga[:], 0.5, ps[:, b + 1, 0:HID],
                                                                      ALU.mult, ALU.mult).then_inc(gb_sb.sem, 1)
                            if not (first and i == 0):
                                result(back(t, 1), i + 1)
                            if i == T - 1 and not last:
                                cut_weight(back(group, -1), 2)
                        if last:
                            hidden_lo(tile_of(group, T - 1))
                            result(tile_of(group, T - 1), T - 1)
                    each_group(dve, work)

                @block.gpsimd
                def _(pool):
                    last_token = pool.to_reg(TOKENS - 1)

                    def cut_weight(group, n):
                        pool.wait_ge(w_hi[n].sem, w_hi[n].at(group))
                        alone(pool)
                        nc.gpsimd.tensor_tensor(out=W[group[1] % 2][n][1][:], in0=raws[n][:],
                                                             in1=W[group[1] % 2][n][0][:].bitcast(F32),
                                                             op=ALU.subtract).then_inc(w_lo[n].sem, 1)

                    def gather(group, i):
                        t = tile_of(group, i)
                        pool.wait_ge(entries_in.of(group), entries_in.at(group))
                        pool.wait_ge(scaled_sb.sem, scaled_sb.at(back(t, 2)))
                        alone(pool)
                        nc.gpsimd.indirect_dma_start(
                            rows[i % 2][:], None, normed, bass.IndirectOffsetOnAxis(
                                ap=entries[group[1] % 2][:, i, 0:1].bitcast(I32), axis=0),
                            bounds_check=last_token, oob_is_err=False).then_inc(rows_in.of(t), 16)

                    def add_rows(group, i):
                        t = tile_of(group, i)
                        pool.wait_ge(res_sb.sem, res_sb.at(t))
                        pool.wait_ge(added.sem, added.at(back(t, 1)))
                        alone(pool)
                        nc.gpsimd.indirect_dma_start(
                            out, bass.IndirectOffsetOnAxis(ap=entries[group[1] % 2][:, i, 0:1].bitcast(I32), axis=0),
                            res[i % 2][:], None, bounds_check=last_token, oob_is_err=False,
                            compute_op=ALU.add).then_inc(added.sem, 16)

                    pool.wait_ge(cleared, 2)

                    def work(group, first, last):
                        if first:
                            gather(group, 0)
                            gather(group, 1)
                            cut_weight(group, 0)
                            cut_weight(group, 1)
                        for i in range(T):
                            if i < T - 2:
                                gather(group, i + 2)
                            elif not last:
                                gather(back(group, -1), i + 2 - T)
                            if i in (1, 2) and not last:
                                cut_weight(back(group, -1), i - 1)
                            if i > 0:
                                add_rows(group, i - 1)
                            elif not first:
                                add_rows(back(group, 1), T - 1)
                        if last:
                            add_rows(group, T - 1)
                            pool.wait_ge(added.sem, added.at(tile_of(group, T - 1)))
                    each_group(pool, work)


_INS = ["x", "L0_attn_Wq", "L0_attn_Wk", "L0_attn_Wv", "L0_attn_Wo", "L0_ffn_gate_w", "L0_ffn_w1", "L0_ffn_w2",
        "L0_ffn_w3", "L0_ffn_sw1", "L0_ffn_sw2", "L0_ffn_sw3", "L0_ffn_expert_bias"]


def rope_tables(tokens, width):
    import numpy as np

    inv_freq = (1.0 / np.float32(10000.0) ** (np.arange(0, width, 2, dtype=np.float32) / np.float32(width))).astype(np.float32)
    freqs = (np.arange(tokens, dtype=np.float32)[:, None] * inv_freq[None, :]).astype(np.float32)
    cos, sin = np.cos(freqs).astype(np.float32), np.sin(freqs).astype(np.float32)
    return np.concatenate([cos, cos], 1), np.concatenate([-sin, sin], 1)


def kernel(**inputs):
    import numpy as np
    import concourse.bacc as bacc
    from concourse import mybir as _mybir
    from concourse.bass_utils import run_bass_kernel_spmd

    nc = bacc.Bacc("TRN2", target_bir_lowering=False, num_devices=1)
    arrays, args = {}, []
    for name in _INS:
        arrays[f"in_{name}"] = np.ascontiguousarray(inputs[name])
    nb, c3, d = inputs["x"].shape
    arrays["rope_cos"], arrays["rope_sin"] = rope_tables(c3 // 3, 64)
    for name, a in arrays.items():
        args.append(nc.dram_tensor(name, a.shape, _mybir.dt.from_np(a.dtype), kind="ExternalInput").ap())
    out = nc.dram_tensor("out_dram", (nb * (c3 // 3), d), _mybir.dt.float32, kind="ExternalOutput").ap()
    audio_tower(nc, *args, out)
    r = run_bass_kernel_spmd(nc, [arrays], core_ids=[0])
    return r.results[0]["out_dram"].reshape(nb, c3 // 3, d)
```
